# Optimizing a Trainium2 kernel written in Bass

```python
import numpy as np
import jax
import jax.numpy as jnp

def _softmax(x, axis=-1):
    return jax.nn.softmax(x, axis=axis)
def _gelu(x):
    return jax.nn.gelu(x, approximate=True)
def _silu(x):
    return jax.nn.silu(x)
def _sigmoid(x):
    return jax.nn.sigmoid(x)
def _layernorm(x, axis=-1, eps=1e-5):
    m = jnp.mean(x, axis=axis, keepdims=True)
    v = jnp.var(x, axis=axis, keepdims=True)
    return (x - m) / jnp.sqrt(v + eps)
def _scatter_add(tgt, idx, src, axis=0):
    return tgt.at[idx].add(src)
def _segment_sum(src, seg, n):
    return jax.ops.segment_sum(src, seg, n)

kernel_name = 'mk_conv_preact_d2_conv_nchw384_f32d79'

def setup_inputs(seed: int = 0):
    np.random.seed(seed)
    _w = jnp.asarray
    def _rec_inputs():
        import jax
        import jax.numpy as jnp
        _gk = jax.random.key(seed)
        x = -0.0001538 + 1 * jax.random.normal(jax.random.fold_in(_gk, 1), (16, 384, 32, 32), jnp.float32)
        return x
    x = _rec_inputs()
    def _L0_conv_setup():
        import jax, jax.numpy as jnp
        import numpy as np
        DIM = 384
        DIM_HEAD = 32
        NUM_HEAD = DIM // DIM_HEAD
        SCALE = DIM_HEAD ** (-0.5)
        key = jax.random.key(seed)
        k1, k2, k3, k4 = jax.random.split(key, 4)
        x = jax.random.normal(k1, (16, DIM, 32, 32), dtype=jnp.float32)
        qkv_w = jax.random.normal(k2, (3 * DIM, DIM), dtype=jnp.float32) * DIM ** (-0.5)
        proj_w = jax.random.normal(k3, (DIM, DIM), dtype=jnp.float32) * DIM ** (-0.5)
        proj_b = jax.random.normal(k4, (DIM,), dtype=jnp.float32) * 0.01
        return {'x': x, 'qkv_w': qkv_w, 'proj_w': proj_w, 'proj_b': proj_b}
    _L0_conv_all = _L0_conv_setup()
    _L0_conv_in = {k: v for k, v in _L0_conv_all.items() if k in ('qkv_w', 'proj_w', 'proj_b', )}
    del _L0_conv_all

    def _L1_conv_setup():
        import jax, jax.numpy as jnp
        import numpy as np
        from jax import lax
        PLANES = 384
        N_POINTS = 4
        KERNEL_SIZE = 11
        INIT_RADIUS = 2.0 * (2.0 / KERNEL_SIZE)

        def _make_kernels(weight_coord, radius, weights):
            K = KERNEL_SIZE
            lin = jnp.linspace(-1.0, 1.0, K)
            gy, gx = jnp.meshgrid(lin, lin, indexing='ij')
            kernel_coord = jnp.stack([gy, gx], axis=0).reshape(2, K * K)
            diff = weight_coord[:, :, None, :] - kernel_coord.T[None, None, :, :]
            diff = jnp.transpose(diff, (0, 1, 3, 2)).reshape(1, N_POINTS, 2, K, K)
            d = jax.nn.relu(1.0 - jnp.abs(diff).sum(axis=2) / radius)
            kernels = jnp.matmul(weights, d.reshape(1, N_POINTS, K * K)).reshape(PLANES, K, K)
            kernels = jnp.flip(jnp.transpose(kernels, (0, 2, 1)), axis=1)
            return kernels
        key = jax.random.key(seed)
        k1, k2, k3 = jax.random.split(key, 3)
        x = jax.random.normal(k1, (16, PLANES, 64, 64), dtype=jnp.float32)
        weight_coord = jnp.clip(0.2 * jax.random.normal(k2, (1, N_POINTS, 2), dtype=jnp.float32), -1.0, 1.0)
        radius = jnp.full((1, N_POINTS, 1, 1), INIT_RADIUS, dtype=jnp.float32)
        weights = 0.02 * jax.random.normal(k3, (1, PLANES, N_POINTS), dtype=jnp.float32)
        return {'x': x, 'weight_coord': weight_coord, 'radius': radius, 'weights': weights}
    _L1_conv_all = _L1_conv_setup()
    _L1_conv_in = {k: v for k, v in _L1_conv_all.items() if k in ('weight_coord', 'radius', 'weights', )}
    del _L1_conv_all

    return {
        "x": x,
        "L0_conv_qkv_w": _L0_conv_in["qkv_w"],
        "L0_conv_proj_w": _L0_conv_in["proj_w"],
        "L0_conv_proj_b": _L0_conv_in["proj_b"],
        "L1_conv_weight_coord": _L1_conv_in["weight_coord"],
        "L1_conv_radius": _L1_conv_in["radius"],
        "L1_conv_weights": _L1_conv_in["weights"],
    }

def reference(x, L0_conv_qkv_w, L0_conv_proj_w, L0_conv_proj_b, L1_conv_weight_coord, L1_conv_radius, L1_conv_weights):
    import jax
    import jax.numpy as jnp
    def _L0_conv_ref(x, qkv_w, proj_w, proj_b):
        import jax, jax.numpy as jnp
        import numpy as np
        DIM = 384
        DIM_HEAD = 32
        NUM_HEAD = DIM // DIM_HEAD
        SCALE = DIM_HEAD ** (-0.5)
        B, C, H, W = x.shape
        N = H * W
        xt = x.reshape(B, C, N).transpose(0, 2, 1)
        qkv = jnp.einsum('bnc,oc->bno', xt, qkv_w)
        qkv = qkv.reshape(B, N, 3, NUM_HEAD, DIM_HEAD).transpose(2, 0, 3, 1, 4)
        q, k, v = (qkv[0], qkv[1], qkv[2])
        attn = jnp.einsum('bhnd,bhmd->bhnm', q, k) * SCALE
        attn = jax.nn.softmax(attn, axis=-1)
        out = jnp.einsum('bhnm,bhmd->bhnd', attn, v)
        out = out.transpose(0, 2, 1, 3).reshape(B, N, C)
        out = jnp.einsum('bnc,oc->bno', out, proj_w) + proj_b
        return out.transpose(0, 2, 1).reshape(B, C, H, W)

    def _L1_conv_ref(x, weight_coord, radius, weights):
        import jax, jax.numpy as jnp
        import numpy as np
        from jax import lax
        PLANES = 384
        N_POINTS = 4
        KERNEL_SIZE = 11
        INIT_RADIUS = 2.0 * (2.0 / KERNEL_SIZE)

        def _make_kernels(weight_coord, radius, weights):
            K = KERNEL_SIZE
            lin = jnp.linspace(-1.0, 1.0, K)
            gy, gx = jnp.meshgrid(lin, lin, indexing='ij')
            kernel_coord = jnp.stack([gy, gx], axis=0).reshape(2, K * K)
            diff = weight_coord[:, :, None, :] - kernel_coord.T[None, None, :, :]
            diff = jnp.transpose(diff, (0, 1, 3, 2)).reshape(1, N_POINTS, 2, K, K)
            d = jax.nn.relu(1.0 - jnp.abs(diff).sum(axis=2) / radius)
            kernels = jnp.matmul(weights, d.reshape(1, N_POINTS, K * K)).reshape(PLANES, K, K)
            kernels = jnp.flip(jnp.transpose(kernels, (0, 2, 1)), axis=1)
            return kernels
        kernels = _make_kernels(weight_coord, radius, weights)
        pad = KERNEL_SIZE // 2
        out = lax.conv_general_dilated(x, kernels[:, None, :, :], window_strides=(1, 1), padding=[(pad, pad), (pad, pad)], dimension_numbers=('NCHW', 'OIHW', 'NCHW'), feature_group_count=PLANES)
        return out

    def _gn(v, G=32, eps=1e-5):
        B_, C_, H_, W_ = v.shape
        g = v.reshape(B_, G, C_ // G, H_, W_)
        m = jnp.mean(g, axis=(2, 3, 4), keepdims=True)
        s = jnp.var(g, axis=(2, 3, 4), keepdims=True)
        return ((g - m) / jnp.sqrt(s + eps)).reshape(v.shape)

    def _ln_c(v, eps=1e-6):
        m = jnp.mean(v, axis=1, keepdims=True)
        s = jnp.var(v, axis=1, keepdims=True)
        return (v - m) / jnp.sqrt(s + eps)

    def _ln_t(v, eps=1e-5):
        m = jnp.mean(v, axis=-1, keepdims=True)
        s = jnp.var(v, axis=-1, keepdims=True)
        return (v - m) / jnp.sqrt(s + eps)

    def _to_tokens(v):
        B_, C_, H_, W_ = v.shape
        return v.reshape(B_, C_, H_ * W_).transpose(0, 2, 1)
    def _from_tokens(t, like):
        B_, C_, H_, W_ = like.shape
        return t.transpose(0, 2, 1).reshape(B_, C_, H_, W_)

    x = x + _L0_conv_ref(_gn(x), L0_conv_qkv_w, L0_conv_proj_w, L0_conv_proj_b)
    x = x + _L1_conv_ref(_gn(x), L1_conv_weight_coord, L1_conv_radius, L1_conv_weights)
    return x


_drawn_inputs = setup_inputs


def setup_inputs(seed=0):
    import zlib

    import numpy as np

    out = dict(_drawn_inputs(seed))
    spreads = {'L1_conv_radius': (0.3636363744735718, 0.6)}
    factors = {'L0_conv_proj_b': 6.219}
    for name, (base, spread) in spreads.items():
        noise = np.random.default_rng([zlib.crc32(name.encode()), seed]).standard_normal(out[name].shape)
        drawn = base * np.exp(spread * noise) if base else spread * noise
        out[name] = jnp.asarray(drawn.astype(out[name].dtype))
    for name, factor in factors.items():
        out[name] = (out[name] * factor).astype(out[name].dtype)
    return out
```

```python
from contextlib import ExitStack

import concourse.bass as bass
from concourse import mybir

ALU = mybir.AluOpType
ACT = mybir.ActivationFunctionType
AX = mybir.AxisListType
F32 = mybir.dt.float32
F32R = mybir.dt.float32r

P = 128
BATCHES, C, IMG = 16, 384, 32
TOK = IMG * IMG
CT = C // P
D = 32
HG = 4
GROUPS = C // D // HG
KT = TOK // P
QN = 512
QC = TOK // QN
SCALE = float(D) ** -0.5
EPS = 1e-5
POINTS, KS = 4, 11
PAD = KS // 2
STEPS = QC * KT
SMAX = HG * KT * 2
SMAX_AT = [0, 0, 0] + [5] * 12 + [4]
GN_LINKS = [5, 6]
assert sum(SMAX_AT) == SMAX and len(SMAX_AT) == STEPS


class Batch:

    def __init__(self, n0, engine=None, turn=None, count=None):
        self.n0, self.engine, self.turn, self.count = n0, engine, turn, count

    def plus(self, k):
        return Batch(self.n0 + k, self.engine, self.turn, self.count)

    def exists(self):
        return 0 <= self.n0 < BATCHES

    def looped(self):
        return self.turn is not None

    def rising(self, per_round, c):
        if not self.looped():
            return c
        self.engine.reg_mul(self.count, self.turn, per_round)
        self.engine.reg_add(self.count, self.count, c)
        return self.count

    def of(self, per, c):
        return self.rising(2 * per, per * self.n0 + c)

    def index(self):
        return self.turn * 2 + self.n0 if self.looped() else self.n0


MISC = (
    [("v", 0, t) for t in range(KT)]
    + [("qk2", 0, 0), ("max1", 0, 0)] + [("qk2", 0, i) for i in (1, 2, 3)]
    + [("gn1", -1, 0), ("gn1", -1, 1)]
    + [("conv", -1, (ct, k)) for ct in range(CT) for k in range(10)]
    + [("gn0", 1, 0), ("gn0", 1, 1), ("qk0", 1, 0), ("max2", 0, 0)] + [("qk0", 1, i) for i in (1, 2, 3)]
    + [("qk1", 1, 0), ("max0", 1, 0)] + [("qk1", 1, i) for i in (1, 2, 3)]
    + [("proj", 0, i) for i in range(CT * QC)]
)
MISC_JOBS = [(name, b + off, i) for b in range(-1, BATCHES + 1) for name, off, i in MISC if 0 <= b + off < BATCHES]
MISC_INDEX = {job: at for at, job in enumerate(MISC_JOBS)}


def build(nc, x, out, wqkv, wproj, bproj, gavg, ident, convw, coord, radius, lin_x, band, lin_y):
    x_b = x.rearrange("b (t p) n -> b p t n", p=P)
    out_b = out.rearrange("b (t p) n -> b p t n", p=P)
    with ExitStack() as ctx:
        def sb(name, shape, dt=F32):
            return ctx.enter_context(nc.sbuf_tensor(name, shape, dt))

        def psum(name, shape):
            return ctx.enter_context(nc.psum_tensor(name, shape, F32))

        def sem(name):
            return ctx.enter_context(nc.semaphore(name))

        wqkv_s = sb("wqkv_s", [P, CT, 3 * C])
        wproj_s = sb("wproj_s", [P, CT, C])
        bproj_s = sb("bproj_s", [P, CT])
        gavg_s = sb("gavg_s", [P, CT, C])
        ident_s = sb("ident_s", [P, P])
        convw_s = sb("convw_s", [P, CT, POINTS])
        coord_s = sb("coord_s", [P, 2])
        radius_s = sb("radius_s", [P, 1])
        lin_x_s = sb("lin_x_s", [P, IMG])
        band_s = sb("band_s", [P, IMG])
        lin_y_s = sb("lin_y_s", [P, KS])
        ones_s = sb("ones_s", [P, D])
        halfpow = sb("halfpow", [P, CT])
        tent = sb("tent", [P, KS, IMG])
        carrier = sb("carrier", [P, 1])
        pool_carrier = sb("pool_carrier", [P, CT])
        tmp_x = sb("tmp_x", [P, IMG])
        tmp_y = sb("tmp_y", [P, KS])
        rinv = sb("rinv", [P, 1])
        xin = sb("xin", [P, CT, TOK])
        y = sb("y", [P, CT, TOK])
        stage = sb("stage", [P, 4, TOK], F32R)
        qp = sb("qp", [P, 2, HG, TOK], F32R)
        kp = sb("kp", [P, 2, HG, TOK], F32R)
        v = sb("v", [P, KT, C])
        probs = sb("probs", [P, 2, HG, QN])
        rden = sb("rden", [P, QN])
        attn = sb("attn", [P, GROUPS, TOK])
        zw = sb("zw", [P, IMG, POINTS, IMG])
        z = sb("z", [P, IMG, P])
        halfmax = sb("halfmax", [P, HG * KT, 2])
        negmax = sb("negmax", [P, HG * KT])
        maxrow = sb("maxrow", [HG * KT, P], F32R)
        bst = [sb(f"bst{i}", [P, CT, 2, 6]) for i in range(2)]
        mv = [sb(f"mv{i}", [P, CT, 2]) for i in range(2)]
        gmean = [sb(f"gmean{i}", [P, CT]) for i in range(2)]
        dev = [sb(f"dev{i}", [P, CT]) for i in range(2)]
        spread = [sb(f"spread{i}", [P, CT]) for i in range(2)]
        gvar = [sb(f"gvar{i}", [P, CT]) for i in range(2)]
        rstd = [sb(f"rstd{i}", [P, CT]) for i in range(2)]
        shift = [sb(f"shift{i}", [P, CT]) for i in range(2)]
        wscale = sb("wscale", [P, CT, POINTS])
        wshift = sb("wshift", [P, CT, POINTS])

        score_t = [psum(f"score_t{i}", [P, QN]) for i in range(2)]
        score_m = [psum(f"score_m{i}", [P, QN]) for i in range(2)]
        acc_o = psum("acc_o", [P, QN])
        acc_d = psum("acc_d", [P, QN])
        misc = [psum(f"misc{i}", [P, QN]) for i in range(2)]

        loaded = sem("loaded")
        consts_set = sem("consts_set")
        tent_step = sem("tent_step")
        x_loaded = sem("x_loaded")
        y_loaded = sem("y_loaded")
        stored = sem("stored")
        packed = [sem(f"packed{j}") for j in range(HG)]
        max_placed = sem("max_placed")
        misc_full = sem("misc_full")
        smax_full = sem("smax_full")
        smax_read = sem("smax_read")
        negmax_ready = sem("negmax_ready")
        maxrow_ready = sem("maxrow_ready")
        st_full = sem("st_full")
        exp_done = sem("exp_done")
        pv_done = sem("pv_done")
        rden_ready = sem("rden_ready")
        attn_ready = sem("attn_ready")
        hi_ready = sem("hi_ready")
        lo_ready = sem("lo_ready")
        v_ready = sem("v_ready")
        stats_ready = [sem(f"stats_ready{i}") for i in range(2)]
        gn_step = [sem(f"gn_step{i}") for i in range(2)]
        rstd_ready = [sem(f"rstd_ready{i}") for i in range(2)]
        xn_ready = sem("xn_ready")
        y_ready = sem("y_ready")
        zw_ready = sem("zw_ready")
        z_ready = sem("z_ready")
        out_ready = sem("out_ready")

        def misc_full_by(e, name, n, i=0):
            at = MISC_INDEX[(name, n.n0, i)]
            e.wait_ge(misc_full, n.rising(2 * len(MISC), at + 1))
            return misc[at % 2]

        def misc_bank(e, name, n, i=0):
            at = MISC_INDEX[(name, n.n0, i)]
            if at >= 2:
                before, m0, k = MISC_JOBS[at - 2]
                m = n.plus(m0 - n.n0)
                if before == "v":
                    e.wait_ge(v_ready, m.of(KT, k + 1))
                elif before.startswith("qk"):
                    e.wait_ge(lo_ready, m.of(4 * GROUPS, 4 * int(before[2]) + k + 1))
                elif before.startswith("max"):
                    e.wait_ge(maxrow_ready, m.of(GROUPS, int(before[3]) + 1))
                elif before.startswith("gn"):
                    e.wait_ge(gn_step[int(before[2])], m.of(GN_LINKS[int(before[2])], 2 * k + 2))
                elif before == "proj":
                    e.wait_ge(y_ready, m.of(CT * QC, k + 1))
                elif k[1] < 8:
                    e.wait_ge(z_ready, m.of(8 * CT, 8 * k[0] + k[1] + 1))
                else:
                    e.wait_ge(out_ready, m.of(2 * CT, 2 * k[0] + k[1] - 7))
            return misc[at % 2]

        def group(n, g):
            return lambda per, c=0: n.of(GROUPS * per, g * per + c)

        def slot_of(n, g):
            return (GROUPS * n.n0 + g) % 2

        def first(n, g, before=0):
            return not n.looped() and GROUPS * n.n0 + g <= before - 1

        def run(e, iteration):
            iteration(Batch(-1))
            iteration(Batch(0))
            with e.register("count") as count, e.Fori(0, (BATCHES - 2) // 2) as turn:
                iteration(Batch(1, e, turn, count))
                iteration(Batch(2, e, turn, count))
            iteration(Batch(BATCHES - 1))
            iteration(Batch(BATCHES))

        block = ctx.enter_context(nc.Block())

        @block.sync
        def _(sp):
            for dst, src in ((ident_s, ident), (gavg_s, gavg), (wqkv_s, wqkv), (wproj_s, wproj), (bproj_s, bproj),
                             (convw_s, convw), (coord_s, coord), (radius_s, radius), (lin_x_s, lin_x),
                             (band_s, band), (lin_y_s, lin_y)):
                sp.dma_start(dst[:], src).then_inc(loaded, 16)

            def load_x(n):
                if n.n0 > 0:
                    at = MISC_INDEX[("qk2", n.n0 - 1, 3)] + 1
                    sp.wait_ge(misc_full, n.rising(2 * len(MISC), at))
                sp.dma_start(xin[:], x_b[n.index()]).then_inc(x_loaded, 16)

            def load_y(n):
                if n.n0 > 0:
                    sp.wait_ge(stored, n.of(16 * CT, 0))
                sp.dma_start(y[:], x_b[n.index()]).then_inc(y_loaded, 16)

            def pack(n, g):
                s, gi = slot_of(n, g), group(n, g)
                sp.wait_ge(lo_ready, gi(4, 4))
                if not first(n, g, 2):
                    sp.wait_ge(st_full, gi(STEPS * HG, -STEPS * HG))
                for j in range(HG):
                    rows = slice(D * j, D * j + D)
                    for dst, at, part in ((qp, 0, 0), (kp, 0, 2), (qp, 1, 1), (kp, 1, 2), (qp, 2, 0), (kp, 2, 3)):
                        sp.dma_start(dst[D * at:D * at + D, s, j, :].bitcast(F32), stage[rows, part, :].bitcast(F32)).then_inc(packed[j], 16)

            def place_max(n, g):
                sp.wait_ge(maxrow_ready, group(n, g)(1, 1))
                sp.dma_start(qp[3 * D:3 * D + 1, slot_of(n, g)].bitcast(F32), maxrow[:].bitcast(F32)).then_inc(max_placed, 16)

            def store(n):
                for ct in range(CT):
                    sp.wait_ge(out_ready, n.of(2 * CT, 2 * ct + 2))
                    sp.dma_start(out_b[n.index()][:, ct], y[:, ct]).then_inc(stored, 16)

            def iteration(b):
                if b.exists():
                    place_max(b, 1)
                    pack(b, 2)
                if b.plus(1).exists():
                    load_x(b.plus(1))
                if b.plus(-1).exists():
                    store(b.plus(-1))
                if b.exists():
                    load_y(b)
                    place_max(b, 2)
                if b.plus(1).exists():
                    pack(b.plus(1), 0)
                    place_max(b.plus(1), 0)
                    pack(b.plus(1), 1)

            run(sp, iteration)
            sp.wait_ge(stored, 16 * CT * BATCHES)

        @block.tensor
        def _(pe):
            def values(n):
                pe.wait_ge(xn_ready, n.of(CT, CT))
                for t in range(KT):
                    ps = misc_bank(pe, "v", n, t)
                    for ct in range(CT):
                        mm = pe.matmul(ps[:, 0:C], xin[:, ct, t * P:(t + 1) * P], wqkv_s[:, ct, 2 * C:3 * C],
                                       start=(ct == 0), stop=(ct == CT - 1))
                    mm.then_inc(misc_full, 1)

            def qk(n, g, i):
                if i == 0:
                    pe.wait_ge(xn_ready, n.of(CT, CT))
                col, q = (i // 2) * C + g * P, (i % 2) * QN
                ps = misc_bank(pe, f"qk{g}", n, i)
                for ct in range(CT):
                    mm = pe.matmul(ps[:], wqkv_s[:, ct, col:col + P], xin[:, ct, q:q + QN],
                                   start=(ct == 0), stop=(ct == CT - 1))
                mm.then_inc(misc_full, 1)

            def max_rows(n, g):
                ps = misc_bank(pe, f"max{g}", n)
                pe.wait_ge(negmax_ready, group(n, g)(1, 1))
                pe.transpose(ps[0:HG * KT, 0:P], negmax[:], ident_s[:]).then_inc(misc_full, 1)

            def smax(n, g, k):
                j, t, half, s, gi = k // (2 * KT), k // 2 % KT, k % 2, slot_of(n, g), group(n, g)
                if k % (2 * KT) == 0:
                    pe.wait_ge(packed[j], gi(96, 96))
                if k >= 2 or not first(n, g, 1):
                    pe.wait_ge(smax_read, gi(SMAX, k - 1))
                pe.matmul(score_m[k % 2][:], qp[0:3 * D, s, j, t * P:(t + 1) * P],
                          kp[0:3 * D, s, j, half * QN:(half + 1) * QN], start=True, stop=True).then_inc(smax_full, 1)

            def scores(n, g, step):
                qc, t, s, gi = step // KT, step % KT, slot_of(n, g), group(n, g)
                if step == 0:
                    pe.wait_ge(max_placed, gi(16, 16))
                for j in range(HG):
                    k = step * HG + j
                    if k >= 2 or not first(n, g, 1):
                        pe.wait_ge(exp_done, gi(STEPS * HG, k - 1))
                    pe.matmul(score_t[k % 2][:], kp[0:3 * D + 1, s, j, t * P:(t + 1) * P],
                              qp[0:3 * D + 1, s, j, qc * QN:(qc + 1) * QN], start=True, stop=True).then_inc(st_full, 1)

            def pv(n, g, step):
                qc, t, gi = step // KT, step % KT, group(n, g)
                pe.wait_ge(exp_done, gi(STEPS * HG, (step + 1) * HG))
                if t == 0 and not (first(n, g, 1) and qc == 0):
                    pe.wait_ge(attn_ready, gi(QC, qc))
                if step == 0 and g == 0:
                    pe.wait_ge(v_ready, n.of(KT, KT))
                for acc, own in ((acc_o, True), (acc_d, False)):
                    for j in range(HG):
                        h = g * HG + j
                        w = v[:, t, h * D:(h + 1) * D] if own else ones_s[:]
                        mm = pe.matmul(acc[D * j:D * j + D, :], w, probs[:, step % 2, j, :], start=(t == 0),
                                       stop=(t == KT - 1), tile_position=(0, D * j))
                mm.then_inc(pv_done, 1)

            def attention(n, g, m, mg):
                k = 0
                for step in range(STEPS):
                    if n.exists():
                        scores(n, g, step)
                    todo = SMAX_AT[step] if m.exists() else 0
                    for i in range(todo):
                        smax(m, mg, k + i)
                        if i == todo // 2 and n.exists() and step > 0:
                            pv(n, g, step - 1)
                    if todo == 0 and n.exists() and step > 0:
                        pv(n, g, step - 1)
                    k += todo

            def gn(n, i):
                for part in range(2):
                    ps = misc_bank(pe, f"gn{i}", n, part)
                    pe.wait_ge(stats_ready[i], n.of(2, part + 1))
                    for ct in range(CT):
                        for k in range(CT):
                            rhs = mv[i][:, k, 0:1] if part == 0 else spread[i][:, k:k + 1]
                            mm = pe.matmul(ps[:, ct:ct + 1], gavg_s[:, k, ct * P:(ct + 1) * P], rhs,
                                           start=(k == 0), stop=(k == CT - 1))
                    mm.then_inc(misc_full, 1)

            def conv(n):
                for ct in range(CT):
                    pe.wait_ge(zw_ready, n.of(CT * POINTS, (ct + 1) * POINTS))
                    for k in range(8):
                        ps = misc_bank(pe, "conv", n, (ct, k))
                        for r in range(4):
                            mm = pe.transpose(ps[:, r * P:(r + 1) * P],
                                              zw[:, 4 * k + r].rearrange("c p x -> c (p x)"), ident_s[:])
                        mm.then_inc(misc_full, 1)
                    for half in range(2):
                        lo, hi = half * IMG // 2, (half + 1) * IMG // 2
                        ps = misc_bank(pe, "conv", n, (ct, 8 + half))
                        rows = range(max(0, lo - PAD), min(IMG, hi + PAD))
                        for row in rows:
                            if row % 4 == 0 or row == rows[0]:
                                pe.wait_ge(z_ready, n.of(CT * 8, ct * 8 + row // 4 + 1))
                            a, e = max(row - PAD, lo), min(row + PAD + 1, hi)
                            dy = a - (row - PAD)
                            mm = pe.matmul(ps[:, (a - lo) * IMG:(e - lo) * IMG], z[:, row, :],
                                           tent[:, dy:dy + e - a, :], start=(row == rows[0]), stop=(row == rows[-1]),
                                           skip_group_check=True)
                        mm.then_inc(misc_full, 1)

            def proj(n):
                for i in range(CT * QC):
                    ot, qc = i % CT, i // CT
                    ps = misc_bank(pe, "proj", n, i)
                    if ot == 0:
                        pe.wait_ge(attn_ready, n.of(GROUPS * QC, (GROUPS - 1) * QC + qc + 1))
                    for g in range(GROUPS):
                        mm = pe.matmul(ps[:], wproj_s[:, g, ot * P:(ot + 1) * P], attn[:, g, qc * QN:(qc + 1) * QN],
                                       start=(g == 0), stop=(g == GROUPS - 1))
                    mm.then_inc(misc_full, 1)

            pe.wait_ge(loaded, 16 * 11)
            pe.wait_ge(consts_set, 1)
            pe.wait_ge(tent_step, 8)

            def iteration(b):
                prev, nxt = b.plus(-1), b.plus(1)
                if b.exists():
                    values(b)
                    attention(b, 0, b, 1)
                    qk(b, 2, 0)
                    max_rows(b, 1)
                    pv(b, 0, STEPS - 1)
                    for i in (1, 2, 3):
                        qk(b, 2, i)
                if prev.exists():
                    gn(prev, 1)
                    conv(prev)
                if b.exists():
                    attention(b, 1, b, 2)
                if nxt.exists():
                    gn(nxt, 0)
                    qk(nxt, 0, 0)
                if b.exists():
                    max_rows(b, 2)
                    pv(b, 1, STEPS - 1)
                if nxt.exists():
                    for i in (1, 2, 3):
                        qk(nxt, 0, i)
                attention(b, 2, nxt, 0)
                if nxt.exists():
                    qk(nxt, 1, 0)
                    max_rows(nxt, 0)
                if b.exists():
                    pv(b, 2, STEPS - 1)
                if nxt.exists():
                    for i in (1, 2, 3):
                        qk(nxt, 1, i)
                if b.exists():
                    proj(b)

            run(pe, iteration)

        @block.scalar
        def _(act):
            def values(n):
                for t in range(KT):
                    ps = misc_full_by(act, "v", n, t)
                    if t == 0 and n.n0 > 0:
                        act.wait_ge(pv_done, n.of(GROUPS * STEPS, 0))
                    act.copy(v[:, t, :], ps[:, 0:C]).then_inc(v_ready, 1)

            def high(n, g, i):
                ps = misc_full_by(act, f"qk{g}", n, i)
                if i == 0 and not first(n, g, 1):
                    for j in range(HG):
                        act.wait_ge(packed[j], group(n, g)(96))
                act.copy(stage[:, 2 * (i // 2), (i % 2) * QN:(i % 2 + 1) * QN], ps[:]).then_inc(hi_ready, 1)

            def exps(n, g):
                gi = group(n, g)
                for k in range(STEPS * HG):
                    step, j = k // HG, k % HG
                    act.wait_ge(st_full, gi(STEPS * HG, k + 1))
                    if j == 0 and not (first(n, g, 1) and step < 2):
                        act.wait_ge(pv_done, gi(STEPS, step - 1))
                    act.activation(probs[:, step % 2, j, :], score_t[k % 2][:], ACT.Exp,
                                   scale=SCALE).then_inc(exp_done, 1)

            def z_rows(n):
                for ct in range(CT):
                    for k in range(8):
                        ps = misc_full_by(act, "conv", n, (ct, k))
                        act.copy(z[:, 4 * k:4 * k + 4, :], ps[:].rearrange("q (y c) -> q y c", c=P)).then_inc(z_ready, 1)

            def iteration(b):
                prev, nxt = b.plus(-1), b.plus(1)
                if b.exists():
                    values(b)
                    exps(b, 0)
                    for i in range(4):
                        high(b, 2, i)
                if prev.exists():
                    z_rows(prev)
                if b.exists():
                    exps(b, 1)
                if nxt.exists():
                    for i in range(4):
                        high(nxt, 0, i)
                if b.exists():
                    exps(b, 2)
                if nxt.exists():
                    for i in range(4):
                        high(nxt, 1, i)

            run(act, iteration)

        @block.gpsimd
        def _(pool):
            def rstd_of(n, i):
                pool.wait_ge(gn_step[i], n.of(GN_LINKS[i], 4))
                pool.tensor_tensor(rstd[i][:], gvar[i][:], halfpow[:], ALU.pow).then_inc(rstd_ready[i], 1)

            def weigh(n):
                pool.wait_ge(gn_step[1], n.of(GN_LINKS[1], 6))
                for ct in range(CT):
                    if ct == 0:
                        if n.n0 > 0:
                            at = MISC_INDEX[("conv", n.n0 - 1, (CT - 1, 7))] + 1
                            pool.wait_ge(misc_full, n.rising(2 * len(MISC), at))
                    else:
                        at = MISC_INDEX[("conv", n.n0, (ct - 1, 7))] + 1
                        pool.wait_ge(misc_full, n.rising(2 * len(MISC), at))
                    pool.tensor_tensor(pool_carrier[:], halfpow[:], halfpow[:], ALU.add)
                    for p in range(POINTS):
                        pool.tensor_scalar(zw[:, :, p, :], y[:, ct].rearrange("c (y x) -> c y x", x=IMG),
                                           wscale[:, ct, p:p + 1], wshift[:, ct, p:p + 1], ALU.mult,
                                           ALU.add).then_inc(zw_ready, 1)

            pool.wait_ge(consts_set, 1)

            def iteration(b):
                prev, nxt = b.plus(-1), b.plus(1)
                if prev.exists():
                    rstd_of(prev, 1)
                    weigh(prev)
                if nxt.exists():
                    rstd_of(nxt, 0)

            run(pool, iteration)

        @block.vector
        def _(dve):
            def link(ins, step, count):
                ins.then_inc(step, 1)
                dve.wait_ge(step, count)

            dve.memset(halfpow[:], -0.5)
            dve.memset(kp[3 * D:3 * D + 1].bitcast(F32), 1.0)
            dve.memset(ones_s[:], 1.0).then_inc(consts_set, 1)
            dve.wait_ge(loaded, 16 * 11)
            link(dve.tensor_scalar(tmp_x[:], lin_x_s[:], coord_s[:, 0:1], None, ALU.subtract), tent_step, 1)
            link(dve.scalar_tensor_tensor(out=tmp_x[:], in0=tmp_x[:], scalar=-1.0, in1=tmp_x[:],
                                          op0=ALU.mult, op1=ALU.max), tent_step, 2)
            link(dve.tensor_scalar(tmp_y[:], lin_y_s[:], coord_s[:, 1:2], None, ALU.subtract), tent_step, 3)
            link(dve.scalar_tensor_tensor(out=tmp_y[:], in0=tmp_y[:], scalar=-1.0, in1=tmp_y[:],
                                          op0=ALU.mult, op1=ALU.max), tent_step, 4)
            link(dve.reciprocal(rinv[:], radius_s[:]), tent_step, 5)
            link(dve.tensor_tensor(tent[:], tmp_x[:].unsqueeze(1).to_broadcast([P, KS, IMG]),
                                   tmp_y[:].unsqueeze(2).to_broadcast([P, KS, IMG]), ALU.add), tent_step, 6)
            link(dve.tensor_scalar(tent[:], tent[:], rinv[:], -1.0, ALU.mult, ALU.add), tent_step, 7)
            link(dve.scalar_tensor_tensor(out=tent[:], in0=tent[:], scalar=0.0,
                                          in1=band_s[:].unsqueeze(1).to_broadcast([P, KS, IMG]),
                                          op0=ALU.min, op1=ALU.mult), tent_step, 8)

            def stats(n, i):
                src = xin if i == 0 else y
                if i == 0:
                    dve.wait_ge(x_loaded, n.of(16, 16))
                else:
                    dve.wait_ge(y_ready, n.of(CT * QC, CT * QC))
                for ct in range(CT):
                    for h in range(2):
                        ins = dve.bn_stats(bst[i][:, ct, h, :], src[:, ct, h * QN:(h + 1) * QN])
                link(ins, gn_step[i], n.of(GN_LINKS[i], 1))
                dve.memset(carrier[:], 0.0)
                for ct in range(CT):
                    ins = dve.bn_aggr(mv[i][:, ct, :], bst[i][:, ct].rearrange("c h s -> c (h s)"))
                ins.then_inc(stats_ready[i], 1)

            def norm(n, i):
                ps = misc_full_by(dve, f"gn{i}", n, 0)
                dve.tensor_copy(gmean[i][:], ps[:, 0:CT])
                link(dve.tensor_tensor(dev[i][:], mv[i][:, :, 0], ps[:, 0:CT], ALU.subtract), gn_step[i], n.of(GN_LINKS[i], 2))
                link(dve.tensor_tensor(dev[i][:], dev[i][:], dev[i][:], ALU.mult), gn_step[i], n.of(GN_LINKS[i], 3))
                dve.tensor_tensor(spread[i][:], dev[i][:], mv[i][:, :, 1], ALU.add).then_inc(stats_ready[i], 1)
                ps = misc_full_by(dve, f"gn{i}", n, 1)
                link(dve.tensor_scalar(gvar[i][:], ps[:, 0:CT], EPS, None, ALU.add), gn_step[i], n.of(GN_LINKS[i], 4))
                dve.wait_ge(rstd_ready[i], n.of(1, 1))
                link(dve.scalar_tensor_tensor(out=shift[i][:], in0=gmean[i][:], scalar=-1.0, in1=rstd[i][:],
                                              op0=ALU.mult, op1=ALU.mult), gn_step[i], n.of(GN_LINKS[i], 5))
                if i == 0:
                    for ct in range(CT):
                        dve.tensor_scalar(xin[:, ct], xin[:, ct], rstd[0][:, ct:ct + 1], shift[0][:, ct:ct + 1],
                                          ALU.mult, ALU.add).then_inc(xn_ready, 1)
                else:
                    dve.tensor_tensor(wscale[:], convw_s[:], rstd[1][:].unsqueeze(2).to_broadcast([P, CT, POINTS]), ALU.mult)
                    dve.tensor_tensor(wshift[:], convw_s[:], shift[1][:].unsqueeze(2).to_broadcast([P, CT, POINTS]),
                                      ALU.mult).then_inc(gn_step[1], 1)

            def read_max(n, g, k):
                dve.wait_ge(smax_full, group(n, g)(SMAX, k + 1))
                dve.tensor_reduce(halfmax[:, k // 2, k % 2:k % 2 + 1], score_m[k % 2][:], AX.X,
                                  ALU.max).then_inc(smax_read, 1)

            def combine_max(n, g):
                dve.wait_ge(smax_read, group(n, g)(SMAX, SMAX))
                dve.tensor_reduce(negmax[:], halfmax[:], AX.X, ALU.max, negate=True).then_inc(negmax_ready, 1)

            def max_rows(n, g):
                ps = misc_full_by(dve, f"max{g}", n)
                if not first(n, g, 1):
                    dve.wait_ge(max_placed, group(n, g)(16))
                dve.tensor_copy(maxrow[:], ps[0:HG * KT, 0:P]).then_inc(maxrow_ready, 1)

            def normalise(n, g, qc):
                gi = group(n, g)
                dve.wait_ge(pv_done, gi(STEPS, (qc + 1) * KT))
                dve.reciprocal(rden[:], acc_d[:]).then_inc(rden_ready, 1)
                dve.wait_ge(rden_ready, gi(QC, qc + 1))
                dve.tensor_tensor(attn[:, g, qc * QN:(qc + 1) * QN], acc_o[:], rden[:], ALU.mult).then_inc(attn_ready, 1)

            def attention(n, g, m, mg):
                k = 0
                for step in range(STEPS):
                    if m.exists():
                        for i in range(SMAX_AT[step]):
                            read_max(m, mg, k + i)
                        k += SMAX_AT[step]
                    if n.exists() and step == KT:
                        normalise(n, g, 0)
                if m.exists():
                    combine_max(m, mg)

            def low(n, g, i):
                bank = MISC_INDEX[(f"qk{g}", n.n0, i)] % 2
                part = stage[:, 2 * (i // 2):2 * (i // 2) + 2, (i % 2) * QN:(i % 2 + 1) * QN]
                dve.wait_ge(hi_ready, group(n, g)(4, i + 1))
                dve.tensor_tensor(part[:, 1], misc[bank][:], part[:, 0].bitcast(F32), ALU.subtract).then_inc(lo_ready, 1)

            def residual(n):
                dve.wait_ge(y_loaded, n.of(16, 16))
                for i in range(CT * QC):
                    ot, qc = i % CT, i // CT
                    ps = misc_full_by(dve, "proj", n, i)
                    part = y[:, ot, qc * QN:(qc + 1) * QN]
                    dve.scalar_tensor_tensor(out=part, in0=ps[:], scalar=bproj_s[:, ot:ot + 1], in1=part,
                                             op0=ALU.add, op1=ALU.add).then_inc(y_ready, 1)

            def outputs(n):
                dve.wait_ge(zw_ready, n.of(CT * POINTS, POINTS))
                for ct in range(CT):
                    for half in range(2):
                        ps = misc_full_by(dve, "conv", n, (ct, 8 + half))
                        part = y[:, ct, half * QN:(half + 1) * QN]
                        dve.tensor_tensor(part, ps[:], part, ALU.add).then_inc(out_ready, 1)

            def iteration(b):
                prev, nxt = b.plus(-1), b.plus(1)
                if b.exists():
                    attention(b, 0, b, 1)
                    low(b, 2, 0)
                    max_rows(b, 1)
                    normalise(b, 0, 1)
                    for i in (1, 2, 3):
                        low(b, 2, i)
                if prev.exists():
                    norm(prev, 1)
                    outputs(prev)
                if b.exists():
                    attention(b, 1, b, 2)
                if nxt.exists():
                    stats(nxt, 0)
                    norm(nxt, 0)
                    low(nxt, 0, 0)
                if b.exists():
                    max_rows(b, 2)
                    normalise(b, 1, 1)
                if nxt.exists():
                    for i in (1, 2, 3):
                        low(nxt, 0, i)
                attention(b, 2, nxt, 0)
                if nxt.exists():
                    low(nxt, 1, 0)
                    max_rows(nxt, 0)
                if b.exists():
                    normalise(b, 2, 1)
                if nxt.exists():
                    for i in (1, 2, 3):
                        low(nxt, 1, i)
                if b.exists():
                    residual(b)
                    stats(b, 1)

            run(dve, iteration)


def kernel(x, L0_conv_qkv_w, L0_conv_proj_w, L0_conv_proj_b, L1_conv_weight_coord, L1_conv_radius, L1_conv_weights):
    import numpy as np
    import concourse.bacc as bacc
    from concourse.bass_utils import run_bass_kernel_spmd

    def tiled(w):
        w = np.asarray(w)
        return np.ascontiguousarray(w.reshape(CT, P, -1).transpose(1, 0, 2))

    lin = np.linspace(-1.0, 1.0, KS).astype(np.float32)
    delta = np.arange(IMG)[:, None] - np.arange(IMG)[None, :] + PAD
    inside = (delta >= 0) & (delta < KS)
    norm_group = np.arange(C) // (C // 32)
    arrays = {
        "x": np.ascontiguousarray(np.asarray(x).reshape(BATCHES, C, TOK)),
        "wqkv": tiled(np.asarray(L0_conv_qkv_w).T),
        "wproj": tiled(np.asarray(L0_conv_proj_w).T),
        "bproj": np.ascontiguousarray(np.asarray(L0_conv_proj_b).reshape(CT, P).T),
        "gavg": tiled((norm_group[:, None] == norm_group[None, :]).astype(np.float32) / np.float32(C // 32)),
        "ident": np.eye(P, dtype=np.float32),
        "convw": tiled(np.asarray(L1_conv_weights)[0]),
        "coord": np.repeat(np.asarray(L1_conv_weight_coord)[0], IMG, axis=0),
        "radius": np.repeat(np.asarray(L1_conv_radius).reshape(POINTS, 1), IMG, axis=0),
        "lin_x": np.tile(lin[np.clip(delta, 0, KS - 1)], (POINTS, 1)),
        "band": np.tile(-inside.astype(np.float32), (POINTS, 1)),
        "lin_y": np.tile(lin, (P, 1)),
    }
    nc = bacc.Bacc("TRN2", target_bir_lowering=False, num_devices=1)
    given = {k: nc.dram_tensor(f"in_{k}", a.shape, F32, kind="ExternalInput").ap() for k, a in arrays.items()}
    out = nc.dram_tensor("out_y", (BATCHES, C, TOK), F32, kind="ExternalOutput").ap()
    build(nc, out=out, **given)
    r = run_bass_kernel_spmd(nc, [{f"in_{k}": a for k, a in arrays.items()}], core_ids=[0])
    return r.results[0]["out_y"].reshape(BATCHES, C, IMG, IMG)
```

```python
from contextlib import ExitStack

import concourse.bass as bass
from concourse import mybir

ALU = mybir.AluOpType
ACT = mybir.ActivationFunctionType
AX = mybir.AxisListType
F32 = mybir.dt.float32
F32R = mybir.dt.float32r

P = 128
BATCHES, C, IMG = 16, 384, 32
TOK = IMG * IMG
CT = C // P
D = 32
HG = 4
GROUPS = C // D // HG
KT = TOK // P
QN = 512
QC = TOK // QN
SCALE = float(D) ** -0.5
EPS = 1e-5
POINTS, KS = 4, 11
PAD = KS // 2
STEPS = QC * KT
SMAX = HG * KT * 2
SMAX_AT = [4] * STEPS
SMAX_LATE = [0, 0, 4, 4] + [5] * 8 + [4] * 4
CHUNK_ROWS = 4
CHUNKS = CT * IMG // CHUNK_ROWS
Z_RING = 3
ZW_ROWS = 8
PIECES = CT * IMG // ZW_ROWS
GN_PE = [(8, 11), (2, 5)]
GN_DVE = [(6, 9, 12, 13), (None, 3, 6, 7)]
GN_LINKS = [5, 6]
assert sum(SMAX_AT) == sum(SMAX_LATE) == SMAX and len(SMAX_LATE) == STEPS


class Batch:

    def __init__(self, n0, engine=None, turn=None, count=None):
        self.n0, self.engine, self.turn, self.count = n0, engine, turn, count

    def plus(self, k):
        return Batch(self.n0 + k, self.engine, self.turn, self.count)

    def exists(self):
        return 0 <= self.n0 < BATCHES

    def looped(self):
        return self.turn is not None

    def rising(self, per_round, c):
        if not self.looped():
            return c
        self.engine.reg_mul(self.count, self.turn, per_round)
        self.engine.reg_add(self.count, self.count, c)
        return self.count

    def of(self, per, c):
        return self.rising(2 * per, per * self.n0 + c)

    def index(self):
        return self.turn * 2 + self.n0 if self.looped() else self.n0


MISC = (
    [("v", 0, t) for t in range(KT)]
    + [("gn1", -1, 0), ("gn1", -1, 1)]
    + [("qk2", 0, 0), ("max1", 0, 0)] + [("qk2", 0, i) for i in (1, 2, 3)]
    + [("z", -1, c) for c in range(CHUNKS)]
    + [("gn0", 1, 0), ("gn0", 1, 1), ("qk0", 1, 0), ("max2", 0, 0)] + [("qk0", 1, i) for i in (1, 2, 3)]
    + [("qk1", 1, 0), ("max0", 1, 0)] + [("qk1", 1, i) for i in (1, 2, 3)]
    + [("proj", 0, i) for i in range(CT * QC)]
)
MISC_JOBS = [(name, b + off, i) for b in range(-1, BATCHES + 1) for name, off, i in MISC if 0 <= b + off < BATCHES]
MISC_INDEX = {job: at for at, job in enumerate(MISC_JOBS)}


def build(nc, x, out, wqkv, wproj, bproj, gavg, ident, convw, coord, radius, lin_x, band, lin_y):
    x_b = x.rearrange("b (t p) n -> b p t n", p=P)
    out_b = out.rearrange("b (t p) n -> b p t n", p=P)
    with ExitStack() as ctx:
        def sb(name, shape, dt=F32):
            return ctx.enter_context(nc.sbuf_tensor(name, shape, dt))

        def psum(name, shape):
            return ctx.enter_context(nc.psum_tensor(name, shape, F32))

        def sem(name):
            return ctx.enter_context(nc.semaphore(name))

        wqkv_s = sb("wqkv_s", [P, CT, 3 * C])
        wproj_s = sb("wproj_s", [P, CT, C])
        bproj_s = sb("bproj_s", [P, CT])
        gavg_s = sb("gavg_s", [P, CT, C])
        ident_s = sb("ident_s", [P, P])
        convw_s = sb("convw_s", [P, CT, POINTS])
        coord_s = sb("coord_s", [P, 2])
        radius_s = sb("radius_s", [P, 1])
        lin_x_s = sb("lin_x_s", [P, IMG])
        band_s = sb("band_s", [P, IMG])
        lin_y_s = sb("lin_y_s", [P, KS])
        ones_s = sb("ones_s", [P, D])
        halfpow = sb("halfpow", [P, CT])
        tent = sb("tent", [P, KS, IMG])
        tent_hi = sb("tent_hi", [P, KS, IMG], F32R)
        tent_lo = sb("tent_lo", [P, KS, IMG], F32R)
        carrier = sb("carrier", [P, 1])
        pool_carrier = sb("pool_carrier", [P, PIECES])
        tmp_x = sb("tmp_x", [P, IMG])
        tmp_y = sb("tmp_y", [P, KS])
        rinv = sb("rinv", [P, 1])
        xin = sb("xin", [P, CT, TOK])
        y = sb("y", [P, CT, TOK])
        stage = sb("stage", [P, 4, TOK], F32R)
        qp = sb("qp", [P, 2, HG, TOK], F32R)
        kp = sb("kp", [P, 2, HG, TOK], F32R)
        v = sb("v", [P, KT, C])
        probs = sb("probs", [P, 2, HG, QN])
        rden = sb("rden", [P, QN])
        attn = sb("attn", [P, GROUPS, TOK])
        zw = sb("zw", [P, 2, ZW_ROWS, POINTS, IMG])
        z_hi = sb("z_hi", [P, Z_RING, CHUNK_ROWS, P], F32R)
        z_lo = sb("z_lo", [P, Z_RING, CHUNK_ROWS, P], F32R)
        halfmax = sb("halfmax", [P, HG * KT, 2])
        negmax = sb("negmax", [P, HG * KT])
        maxrow = sb("maxrow", [HG * KT, P], F32R)
        bst = [sb(f"bst{i}", [P, CT, 2, 6]) for i in range(2)]
        mv = [sb(f"mv{i}", [P, CT, 2]) for i in range(2)]
        gmean = [sb(f"gmean{i}", [P, CT]) for i in range(2)]
        dev = [sb(f"dev{i}", [P, CT]) for i in range(2)]
        spread = [sb(f"spread{i}", [P, CT]) for i in range(2)]
        gvar = [sb(f"gvar{i}", [P, CT]) for i in range(2)]
        rstd = [sb(f"rstd{i}", [P, CT]) for i in range(2)]
        shift = [sb(f"shift{i}", [P, CT]) for i in range(2)]
        wscale = sb("wscale", [P, CT, POINTS])
        wshift = sb("wshift", [P, CT, POINTS])

        score_t = [psum(f"score_t{i}", [P, QN]) for i in range(2)]
        score_m = [psum(f"score_m{i}", [P, QN]) for i in range(2)]
        acc_o = psum("acc_o", [P, QN])
        acc_d = psum("acc_d", [P, QN])
        misc = [psum(f"misc{i}", [P, QN]) for i in range(2)]

        loaded = sem("loaded")
        consts_set = sem("consts_set")
        tent_step = sem("tent_step")
        x_loaded = sem("x_loaded")
        y_loaded = sem("y_loaded")
        stored = sem("stored")
        packed = [sem(f"packed{j}") for j in range(HG)]
        max_placed = sem("max_placed")
        misc_full = sem("misc_full")
        smax_full = sem("smax_full")
        smax_read = sem("smax_read")
        negmax_ready = sem("negmax_ready")
        maxrow_ready = sem("maxrow_ready")
        st_full = sem("st_full")
        exp_done = sem("exp_done")
        pv_done = sem("pv_done")
        rden_ready = sem("rden_ready")
        attn_ready = sem("attn_ready")
        hi_ready = sem("hi_ready")
        lo_ready = sem("lo_ready")
        v_ready = sem("v_ready")
        stats_ready = [sem(f"stats_ready{i}") for i in range(2)]
        gn_step = [sem(f"gn_step{i}") for i in range(2)]
        rstd_ready = [sem(f"rstd_ready{i}") for i in range(2)]
        xn_ready = sem("xn_ready")
        y_ready = sem("y_ready")
        zw_ready = sem("zw_ready")
        z_hi_ready = sem("z_hi_ready")
        z_lo_ready = sem("z_lo_ready")
        conv_full = sem("conv_full")
        out_ready = sem("out_ready")

        def misc_full_by(e, name, n, i=0):
            at = MISC_INDEX[(name, n.n0, i)]
            e.wait_ge(misc_full, n.rising(2 * len(MISC), at + 1))
            return misc[at % 2]

        def misc_bank(e, name, n, i=0):
            at = MISC_INDEX[(name, n.n0, i)]
            if at >= 2:
                before, m0, k = MISC_JOBS[at - 2]
                m = n.plus(m0 - n.n0)
                if before == "v":
                    e.wait_ge(v_ready, m.of(KT, k + 1))
                elif before.startswith("qk"):
                    e.wait_ge(lo_ready, m.of(4 * GROUPS, 4 * int(before[2]) + k + 1))
                elif before.startswith("max"):
                    e.wait_ge(maxrow_ready, m.of(GROUPS, int(before[3]) + 1))
                elif before.startswith("gn"):
                    e.wait_ge(gn_step[int(before[2])], m.of(GN_LINKS[int(before[2])], 2 * k + 2))
                elif before == "proj":
                    e.wait_ge(y_ready, m.of(CT * QC, k + 1))
                else:
                    e.wait_ge(z_lo_ready, m.of(CHUNKS, k + 1))
            return misc[at % 2]

        def group(n, g):
            return lambda per, c=0: n.of(GROUPS * per, g * per + c)

        def slot_of(n, g):
            return (GROUPS * n.n0 + g) % 2

        def first(n, g, before=0):
            return not n.looped() and GROUPS * n.n0 + g <= before - 1

        def run(e, iteration):
            iteration(Batch(-1))
            iteration(Batch(0))
            with e.register("count") as count, e.Fori(0, (BATCHES - 2) // 2) as turn:
                iteration(Batch(1, e, turn, count))
                iteration(Batch(2, e, turn, count))
            iteration(Batch(BATCHES - 1))
            iteration(Batch(BATCHES))

        block = ctx.enter_context(nc.Block())

        @block.sync
        def _(sp):
            for dst, src in ((ident_s, ident), (gavg_s, gavg), (wqkv_s, wqkv), (wproj_s, wproj), (bproj_s, bproj),
                             (convw_s, convw), (coord_s, coord), (radius_s, radius), (lin_x_s, lin_x),
                             (band_s, band), (lin_y_s, lin_y)):
                sp.dma_start(dst[:], src).then_inc(loaded, 16)

            def load_x(n):
                if n.n0 > 0:
                    at = MISC_INDEX[("qk2", n.n0 - 1, 3)] + 1
                    sp.wait_ge(misc_full, n.rising(2 * len(MISC), at))
                sp.dma_start(xin[:], x_b[n.index()]).then_inc(x_loaded, 16)

            def load_y(n):
                if n.n0 > 0:
                    sp.wait_ge(stored, n.of(16 * CT, 0))
                sp.dma_start(y[:], x_b[n.index()]).then_inc(y_loaded, 16)

            def pack(n, g):
                s, gi = slot_of(n, g), group(n, g)
                sp.wait_ge(lo_ready, gi(4, 4))
                if not first(n, g, 2):
                    sp.wait_ge(st_full, gi(STEPS * HG, -STEPS * HG))
                for j in range(HG):
                    rows = slice(D * j, D * j + D)
                    for dst, at, part in ((qp, 0, 0), (kp, 0, 2), (qp, 1, 1), (kp, 1, 2), (qp, 2, 0), (kp, 2, 3)):
                        sp.dma_start(dst[D * at:D * at + D, s, j, :].bitcast(F32), stage[rows, part, :].bitcast(F32)).then_inc(packed[j], 16)

            def place_max(n, g):
                sp.wait_ge(maxrow_ready, group(n, g)(1, 1))
                sp.dma_start(qp[3 * D:3 * D + 1, slot_of(n, g)].bitcast(F32), maxrow[:].bitcast(F32)).then_inc(max_placed, 16)

            def store(n):
                for ct in range(CT):
                    sp.wait_ge(out_ready, n.of(2 * CT, 2 * ct + 2))
                    sp.dma_start(out_b[n.index()][:, ct], y[:, ct]).then_inc(stored, 16)

            def iteration(b):
                if b.exists():
                    place_max(b, 1)
                    pack(b, 2)
                if b.plus(1).exists():
                    load_x(b.plus(1))
                if b.plus(-1).exists():
                    store(b.plus(-1))
                if b.exists():
                    load_y(b)
                    place_max(b, 2)
                if b.plus(1).exists():
                    pack(b.plus(1), 0)
                    place_max(b.plus(1), 0)
                    pack(b.plus(1), 1)

            run(sp, iteration)
            sp.wait_ge(stored, 16 * CT * BATCHES)

        @block.tensor
        def _(pe):
            def values(n):
                pe.wait_ge(xn_ready, n.of(CT, CT))
                for t in range(KT):
                    ps = misc_bank(pe, "v", n, t)
                    for ct in range(CT):
                        mm = pe.matmul(ps[:, 0:C], xin[:, ct, t * P:(t + 1) * P], wqkv_s[:, ct, 2 * C:3 * C],
                                       start=(ct == 0), stop=(ct == CT - 1))
                    mm.then_inc(misc_full, 1)

            def qk(n, g, i):
                if i == 0:
                    pe.wait_ge(xn_ready, n.of(CT, CT))
                col, q = (i // 2) * C + g * P, (i % 2) * QN
                ps = misc_bank(pe, f"qk{g}", n, i)
                for ct in range(CT):
                    mm = pe.matmul(ps[:], wqkv_s[:, ct, col:col + P], xin[:, ct, q:q + QN],
                                   start=(ct == 0), stop=(ct == CT - 1))
                mm.then_inc(misc_full, 1)

            def max_rows(n, g):
                ps = misc_bank(pe, f"max{g}", n)
                pe.wait_ge(negmax_ready, group(n, g)(1, 1))
                pe.transpose(ps[0:HG * KT, 0:P], negmax[:], ident_s[:]).then_inc(misc_full, 1)

            def smax(n, g, k):
                j, t, half, s, gi = k // (2 * KT), k // 2 % KT, k % 2, slot_of(n, g), group(n, g)
                if k % (2 * KT) == 0:
                    pe.wait_ge(packed[j], gi(96, 96))
                if k >= 2 or not first(n, g, 1):
                    pe.wait_ge(smax_read, gi(SMAX, k - 1))
                pe.matmul(score_m[k % 2][:], qp[0:3 * D, s, j, t * P:(t + 1) * P],
                          kp[0:3 * D, s, j, half * QN:(half + 1) * QN], start=True, stop=True).then_inc(smax_full, 1)

            def scores(n, g, step, j):
                qc, t, s, gi = step // KT, step % KT, slot_of(n, g), group(n, g)
                k = step * HG + j
                if k == 0:
                    pe.wait_ge(max_placed, gi(16, 16))
                if k >= 2 or not first(n, g, 1):
                    pe.wait_ge(exp_done, gi(STEPS * HG, k - 1))
                pe.matmul(score_t[k % 2][:], kp[0:3 * D + 1, s, j, t * P:(t + 1) * P],
                          qp[0:3 * D + 1, s, j, qc * QN:(qc + 1) * QN], start=True, stop=True).then_inc(st_full, 1)

            def pv(n, g, step, part):
                qc, t, gi = step // KT, step % KT, group(n, g)
                if part == 0:
                    pe.wait_ge(exp_done, gi(STEPS * HG, (step + 1) * HG))
                    if t == 0 and not (first(n, g, 1) and qc == 0):
                        pe.wait_ge(attn_ready, gi(QC, qc))
                    if step == 0 and g == 1 and n.plus(-1).exists():
                        pe.wait_ge(out_ready, n.of(2 * CT, 0))
                    if step == 0 and g == 0:
                        pe.wait_ge(v_ready, n.of(KT, KT))
                for j in range(HG):
                    h = g * HG + j
                    w = v[:, t, h * D:(h + 1) * D] if part == 0 else ones_s[:]
                    mm = pe.matmul((acc_o, acc_d)[part][D * j:D * j + D, :], w, probs[:, step % 2, j, :], start=(t == 0),
                                   stop=(t == KT - 1), tile_position=(0, D * j))
                if part == 1:
                    mm.then_inc(pv_done, 1)

            def attention(n, g, m, mg, between=None):
                k = 0
                for step in range(STEPS):
                    (between or {}).get(step, lambda: None)()
                    todo = (SMAX_LATE if mg == 0 else SMAX_AT)[step] if m.exists() else 0
                    for piece in range(4):
                        if n.exists():
                            if piece in (0, 2):
                                scores(n, g, step, piece)
                                scores(n, g, step, piece + 1)
                            elif step > 0:
                                pv(n, g, step - 1, piece // 2)
                        for i in range((todo - piece + 3) // 4):
                            smax(m, mg, k)
                            k += 1

            def gn(n, i, part):
                ps = misc_bank(pe, f"gn{i}", n, part)
                pe.wait_ge(stats_ready[i], n.of(2, part + 1))
                for ct in range(CT):
                    for k in range(CT):
                        rhs = mv[i][:, k, 0:1] if part == 0 else spread[i][:, k:k + 1]
                        mm = pe.matmul(ps[:, ct:ct + 1], gavg_s[:, k, ct * P:(ct + 1) * P], rhs,
                                       start=(k == 0), stop=(k == CT - 1))
                mm.then_inc(misc_full, 1)

            def gn_between(n, i):
                return {at: (lambda part=part: gn(n, i, part)) for part, at in enumerate(GN_PE[i])} if n.exists() else None

            def turn_chunk(n, c):
                ps = misc_bank(pe, "z", n, c)
                piece, row = c * CHUNK_ROWS // ZW_ROWS, c * CHUNK_ROWS % ZW_ROWS
                if row == 0:
                    pe.wait_ge(zw_ready, n.of(PIECES * POINTS, (piece + 1) * POINTS))
                for r in range(CHUNK_ROWS):
                    mm = pe.transpose(ps[:, r * P:(r + 1) * P], zw[:, piece % 2, row + r].rearrange("c p x -> c (p x)"),
                                      ident_s[:])
                mm.then_inc(misc_full, 1)

            def conv(n):
                turn_chunk(n, 0)
                turn_chunk(n, 1)
                pe.wait_ge(attn_ready, n.plus(1).of(GROUPS * QC, QC if n.plus(1).exists() else 0))
                half_rows = IMG // 2
                for c in range(CHUNKS):
                    if c + 2 < CHUNKS:
                        turn_chunk(n, c + 2)
                    pe.wait_ge(z_lo_ready, n.of(CHUNKS, c + 1))
                    ct, row0 = c * CHUNK_ROWS // IMG, c * CHUNK_ROWS % IMG
                    if row0 == 0 and ct > 0:
                        pe.wait_ge(out_ready, n.of(2 * CT, 2 * ct))
                    for r in range(CHUNK_ROWS):
                        row = row0 + r
                        for half, acc in enumerate((acc_o, acc_d)):
                            lo, hi = half * half_rows, (half + 1) * half_rows
                            a, e = max(row - PAD, lo), min(row + PAD + 1, hi)
                            if a >= e:
                                continue
                            dy = a - (row - PAD)
                            for part, (zp, tp) in enumerate(((z_hi, tent_hi), (z_lo, tent_hi), (z_hi, tent_lo))):
                                mm = pe.matmul(acc[:, (a - lo) * IMG:(e - lo) * IMG], zp[:, c % Z_RING, r, :],
                                               tp[:, dy:dy + e - a, :], start=(row == max(0, lo - PAD) and part == 0),
                                               stop=(row == min(IMG, hi + PAD) - 1 and part == 2), skip_group_check=True)
                            if row == min(IMG, hi + PAD) - 1:
                                mm.then_inc(conv_full, 1)

            def proj(n):
                for i in range(CT * QC):
                    ot, qc = i % CT, i // CT
                    ps = misc_bank(pe, "proj", n, i)
                    if ot == 0:
                        pe.wait_ge(attn_ready, n.of(GROUPS * QC, (GROUPS - 1) * QC + qc + 1))
                    for g in range(GROUPS):
                        mm = pe.matmul(ps[:], wproj_s[:, g, ot * P:(ot + 1) * P], attn[:, g, qc * QN:(qc + 1) * QN],
                                       start=(g == 0), stop=(g == GROUPS - 1))
                    mm.then_inc(misc_full, 1)

            pe.wait_ge(loaded, 16 * 11)
            pe.wait_ge(consts_set, 1)
            pe.wait_ge(tent_step, 10)

            def iteration(b):
                prev, nxt = b.plus(-1), b.plus(1)
                if b.exists():
                    values(b)
                attention(b, 0, b, 1, gn_between(prev, 1))
                if b.exists():
                    qk(b, 2, 0)
                    max_rows(b, 1)
                    pv(b, 0, STEPS - 1, 0)
                    pv(b, 0, STEPS - 1, 1)
                    for i in (1, 2, 3):
                        qk(b, 2, i)
                if prev.exists():
                    conv(prev)
                attention(b, 1, b, 2, gn_between(nxt, 0))
                if nxt.exists():
                    qk(nxt, 0, 0)
                if b.exists():
                    max_rows(b, 2)
                    pv(b, 1, STEPS - 1, 0)
                    pv(b, 1, STEPS - 1, 1)
                if nxt.exists():
                    for i in (1, 2, 3):
                        qk(nxt, 0, i)
                attention(b, 2, nxt, 0)
                if nxt.exists():
                    qk(nxt, 1, 0)
                    max_rows(nxt, 0)
                if b.exists():
                    pv(b, 2, STEPS - 1, 0)
                    pv(b, 2, STEPS - 1, 1)
                if nxt.exists():
                    for i in (1, 2, 3):
                        qk(nxt, 1, i)
                if b.exists():
                    proj(b)

            run(pe, iteration)

        @block.scalar
        def _(act):
            def values(n):
                for t in range(KT):
                    ps = misc_full_by(act, "v", n, t)
                    if t == 0 and n.n0 > 0:
                        act.wait_ge(pv_done, n.of(GROUPS * STEPS, 0))
                    act.copy(v[:, t, :], ps[:, 0:C]).then_inc(v_ready, 1)

            def high(n, g, i):
                ps = misc_full_by(act, f"qk{g}", n, i)
                if i == 0 and not first(n, g, 1):
                    for j in range(HG):
                        act.wait_ge(packed[j], group(n, g)(96))
                act.copy(stage[:, 2 * (i // 2), (i % 2) * QN:(i % 2 + 1) * QN], ps[:]).then_inc(hi_ready, 1)

            def exps(n, g):
                gi = group(n, g)
                for k in range(STEPS * HG):
                    step, j = k // HG, k % HG
                    act.wait_ge(st_full, gi(STEPS * HG, k + 1))
                    if j == 0 and not (first(n, g, 1) and step < 2):
                        act.wait_ge(pv_done, gi(STEPS, step - 1))
                    act.activation(probs[:, step % 2, j, :], score_t[k % 2][:], ACT.Exp,
                                   scale=SCALE).then_inc(exp_done, 1)

            def z_high(n):
                for c in range(CHUNKS):
                    ps = misc_full_by(act, "z", n, c)
                    act.copy(z_hi[:, c % Z_RING], ps[:].rearrange("q (y c) -> q y c", c=P)).then_inc(z_hi_ready, 1)

            def iteration(b):
                prev, nxt = b.plus(-1), b.plus(1)
                if b.exists():
                    values(b)
                    exps(b, 0)
                    for i in range(4):
                        high(b, 2, i)
                if prev.exists():
                    z_high(prev)
                if b.exists():
                    exps(b, 1)
                if nxt.exists():
                    for i in range(4):
                        high(nxt, 0, i)
                if b.exists():
                    exps(b, 2)
                if nxt.exists():
                    for i in range(4):
                        high(nxt, 1, i)

            run(act, iteration)

        @block.gpsimd
        def _(pool):
            def rstd_of(n, i):
                pool.wait_ge(gn_step[i], n.of(GN_LINKS[i], 4))
                pool.tensor_tensor(rstd[i][:], gvar[i][:], halfpow[:], ALU.pow).then_inc(rstd_ready[i], 1)

            def weigh(n):
                pool.wait_ge(gn_step[1], n.of(GN_LINKS[1], 6))
                for piece in range(PIECES):
                    ct, row = piece * ZW_ROWS // IMG, piece * ZW_ROWS % IMG
                    if piece >= 2 or n.n0 > 0:
                        last = ((piece - 1) * ZW_ROWS // CHUNK_ROWS - 1) % CHUNKS
                        at = MISC_INDEX[("z", n.n0 if piece >= 2 else n.n0 - 1, last)] + 1
                        pool.wait_ge(misc_full, n.rising(2 * len(MISC), at))
                    pool.tensor_tensor(pool_carrier[:, piece:piece + 1], halfpow[:, 0:1], halfpow[:, 0:1], ALU.add)
                    for p in range(POINTS):
                        pool.tensor_scalar(zw[:, piece % 2, :, p, :],
                                           y[:, ct, row * IMG:(row + ZW_ROWS) * IMG].rearrange("c (y x) -> c y x", x=IMG),
                                           wscale[:, ct, p:p + 1], wshift[:, ct, p:p + 1], ALU.mult,
                                           ALU.add).then_inc(zw_ready, 1)

            pool.wait_ge(consts_set, 1)

            def iteration(b):
                prev, nxt = b.plus(-1), b.plus(1)
                if prev.exists():
                    rstd_of(prev, 1)
                    weigh(prev)
                if nxt.exists():
                    rstd_of(nxt, 0)

            run(pool, iteration)

        @block.vector
        def _(dve):
            def link(ins, step, count):
                ins.then_inc(step, 1)
                dve.wait_ge(step, count)

            dve.memset(halfpow[:], -0.5)
            dve.memset(kp[3 * D:3 * D + 1].bitcast(F32), 1.0)
            dve.memset(ones_s[:], 1.0).then_inc(consts_set, 1)
            dve.wait_ge(loaded, 16 * 11)
            link(dve.tensor_scalar(tmp_x[:], lin_x_s[:], coord_s[:, 0:1], None, ALU.subtract), tent_step, 1)
            link(dve.scalar_tensor_tensor(out=tmp_x[:], in0=tmp_x[:], scalar=-1.0, in1=tmp_x[:],
                                          op0=ALU.mult, op1=ALU.max), tent_step, 2)
            link(dve.tensor_scalar(tmp_y[:], lin_y_s[:], coord_s[:, 1:2], None, ALU.subtract), tent_step, 3)
            link(dve.scalar_tensor_tensor(out=tmp_y[:], in0=tmp_y[:], scalar=-1.0, in1=tmp_y[:],
                                          op0=ALU.mult, op1=ALU.max), tent_step, 4)
            link(dve.reciprocal(rinv[:], radius_s[:]), tent_step, 5)
            link(dve.tensor_tensor(tent[:], tmp_x[:].unsqueeze(1).to_broadcast([P, KS, IMG]),
                                   tmp_y[:].unsqueeze(2).to_broadcast([P, KS, IMG]), ALU.add), tent_step, 6)
            link(dve.tensor_scalar(tent[:], tent[:], rinv[:], -1.0, ALU.mult, ALU.add), tent_step, 7)
            link(dve.scalar_tensor_tensor(out=tent[:], in0=tent[:], scalar=0.0,
                                          in1=band_s[:].unsqueeze(1).to_broadcast([P, KS, IMG]),
                                          op0=ALU.min, op1=ALU.mult), tent_step, 8)
            link(dve.tensor_copy(tent_hi[:], tent[:]), tent_step, 9)
            dve.tensor_tensor(tent_lo[:], tent[:], tent_hi[:].bitcast(F32), ALU.subtract).then_inc(tent_step, 1)

            def stats(n, i):
                src = xin if i == 0 else y
                if i == 0:
                    dve.wait_ge(x_loaded, n.of(16, 16))
                else:
                    dve.wait_ge(y_ready, n.of(CT * QC, CT * QC))
                for ct in range(CT):
                    for h in range(2):
                        ins = dve.bn_stats(bst[i][:, ct, h, :], src[:, ct, h * QN:(h + 1) * QN])
                link(ins, gn_step[i], n.of(GN_LINKS[i], 1))
                dve.memset(carrier[:], 0.0)
                for ct in range(CT):
                    ins = dve.bn_aggr(mv[i][:, ct, :], bst[i][:, ct].rearrange("c h s -> c (h s)"))
                ins.then_inc(stats_ready[i], 1)

            def norm_mean(n, i):
                ps = misc_full_by(dve, f"gn{i}", n, 0)
                dve.tensor_copy(gmean[i][:], ps[:, 0:CT])
                link(dve.tensor_tensor(dev[i][:], mv[i][:, :, 0], ps[:, 0:CT], ALU.subtract), gn_step[i], n.of(GN_LINKS[i], 2))
                link(dve.tensor_tensor(dev[i][:], dev[i][:], dev[i][:], ALU.mult), gn_step[i], n.of(GN_LINKS[i], 3))
                dve.tensor_tensor(spread[i][:], dev[i][:], mv[i][:, :, 1], ALU.add).then_inc(stats_ready[i], 1)

            def norm_var(n, i):
                ps = misc_full_by(dve, f"gn{i}", n, 1)
                link(dve.tensor_scalar(gvar[i][:], ps[:, 0:CT], EPS, None, ALU.add), gn_step[i], n.of(GN_LINKS[i], 4))

            def norm_scale(n, i):
                dve.wait_ge(rstd_ready[i], n.of(1, 1))
                link(dve.scalar_tensor_tensor(out=shift[i][:], in0=gmean[i][:], scalar=-1.0, in1=rstd[i][:],
                                              op0=ALU.mult, op1=ALU.mult), gn_step[i], n.of(GN_LINKS[i], 5))
                if i == 0:
                    for ct in range(CT):
                        dve.tensor_scalar(xin[:, ct], xin[:, ct], rstd[0][:, ct:ct + 1], shift[0][:, ct:ct + 1],
                                          ALU.mult, ALU.add).then_inc(xn_ready, 1)
                else:
                    dve.tensor_tensor(wscale[:], convw_s[:], rstd[1][:].unsqueeze(2).to_broadcast([P, CT, POINTS]), ALU.mult)
                    dve.tensor_tensor(wshift[:], convw_s[:], shift[1][:].unsqueeze(2).to_broadcast([P, CT, POINTS]),
                                      ALU.mult).then_inc(gn_step[1], 1)

            def read_max(n, g, k):
                dve.wait_ge(smax_full, group(n, g)(SMAX, k + 1))
                dve.tensor_reduce(halfmax[:, k // 2, k % 2:k % 2 + 1], score_m[k % 2][:], AX.X,
                                  ALU.max).then_inc(smax_read, 1)

            def combine_max(n, g):
                dve.wait_ge(smax_read, group(n, g)(SMAX, SMAX))
                dve.tensor_reduce(negmax[:], halfmax[:], AX.X, ALU.max, negate=True).then_inc(negmax_ready, 1)

            def max_rows(n, g):
                ps = misc_full_by(dve, f"max{g}", n)
                if not first(n, g, 1):
                    dve.wait_ge(max_placed, group(n, g)(16))
                dve.tensor_copy(maxrow[:], ps[0:HG * KT, 0:P]).then_inc(maxrow_ready, 1)

            def normalise(n, g, qc):
                gi = group(n, g)
                dve.wait_ge(pv_done, gi(STEPS, (qc + 1) * KT))
                dve.reciprocal(rden[:], acc_d[:]).then_inc(rden_ready, 1)
                dve.wait_ge(rden_ready, gi(QC, qc + 1))
                dve.tensor_tensor(attn[:, g, qc * QN:(qc + 1) * QN], acc_o[:], rden[:], ALU.mult).then_inc(attn_ready, 1)

            def norm_between(n, i):
                parts = (stats, norm_mean, norm_var, norm_scale)
                return {at: (lambda part=part: part(n, i)) for part, at in zip(parts, GN_DVE[i])} if n.exists() else None

            def attention(n, g, m, mg, between=None):
                k = 0
                for step in range(STEPS):
                    (between or {}).get(step, lambda: None)()
                    if m.exists():
                        for i in range((SMAX_LATE if mg == 0 else SMAX_AT)[step]):
                            read_max(m, mg, k + i)
                        k += (SMAX_LATE if mg == 0 else SMAX_AT)[step]
                    if n.exists() and step == KT:
                        normalise(n, g, 0)
                if m.exists():
                    combine_max(m, mg)

            def low(n, g, i):
                bank = MISC_INDEX[(f"qk{g}", n.n0, i)] % 2
                part = stage[:, 2 * (i // 2):2 * (i // 2) + 2, (i % 2) * QN:(i % 2 + 1) * QN]
                dve.wait_ge(hi_ready, group(n, g)(4, i + 1))
                dve.tensor_tensor(part[:, 1], misc[bank][:], part[:, 0].bitcast(F32), ALU.subtract).then_inc(lo_ready, 1)

            def residual(n):
                dve.wait_ge(y_loaded, n.of(16, 16))
                for i in range(CT * QC):
                    ot, qc = i % CT, i // CT
                    ps = misc_full_by(dve, "proj", n, i)
                    part = y[:, ot, qc * QN:(qc + 1) * QN]
                    dve.scalar_tensor_tensor(out=part, in0=ps[:], scalar=bproj_s[:, ot:ot + 1], in1=part,
                                             op0=ALU.add, op1=ALU.add).then_inc(y_ready, 1)

            def z_low(n, c):
                bank = misc[MISC_INDEX[("z", n.n0, c)] % 2]
                dve.wait_ge(z_hi_ready, n.of(CHUNKS, c + 1))
                dve.tensor_tensor(z_lo[:, c % Z_RING], bank[:].rearrange("q (y c) -> q y c", c=P),
                                  z_hi[:, c % Z_RING].bitcast(F32), ALU.subtract).then_inc(z_lo_ready, 1)

            def outputs(n, ct):
                for half, acc in enumerate((acc_o, acc_d)):
                    dve.wait_ge(conv_full, n.of(2 * CT, 2 * ct + half + 1))
                    part = y[:, ct, half * QN:(half + 1) * QN]
                    dve.tensor_tensor(part, acc[:], part, ALU.add).then_inc(out_ready, 1)

            def conv(n):
                for c in range(CHUNKS):
                    z_low(n, c)
                    done = c - 2 - (CHUNKS // CT - 1)
                    if done >= 0 and done % (CHUNKS // CT) == 0:
                        outputs(n, done // (CHUNKS // CT))
                outputs(n, CT - 1)

            def iteration(b):
                prev, nxt = b.plus(-1), b.plus(1)
                attention(b, 0, b, 1, norm_between(prev, 1))
                if b.exists():
                    low(b, 2, 0)
                    max_rows(b, 1)
                    normalise(b, 0, 1)
                    for i in (1, 2, 3):
                        low(b, 2, i)
                if prev.exists():
                    conv(prev)
                attention(b, 1, b, 2, norm_between(nxt, 0))
                if nxt.exists():
                    low(nxt, 0, 0)
                if b.exists():
                    max_rows(b, 2)
                    normalise(b, 1, 1)
                if nxt.exists():
                    for i in (1, 2, 3):
                        low(nxt, 0, i)
                attention(b, 2, nxt, 0)
                if nxt.exists():
                    low(nxt, 1, 0)
                    max_rows(nxt, 0)
                if b.exists():
                    normalise(b, 2, 1)
                if nxt.exists():
                    for i in (1, 2, 3):
                        low(nxt, 1, i)
                if b.exists():
                    residual(b)
                    stats(b, 1)

            run(dve, iteration)


def kernel(x, L0_conv_qkv_w, L0_conv_proj_w, L0_conv_proj_b, L1_conv_weight_coord, L1_conv_radius, L1_conv_weights):
    import numpy as np
    import concourse.bacc as bacc
    from concourse.bass_utils import run_bass_kernel_spmd

    def tiled(w):
        w = np.asarray(w)
        return np.ascontiguousarray(w.reshape(CT, P, -1).transpose(1, 0, 2))

    lin = np.linspace(-1.0, 1.0, KS).astype(np.float32)
    delta = np.arange(IMG)[:, None] - np.arange(IMG)[None, :] + PAD
    inside = (delta >= 0) & (delta < KS)
    norm_group = np.arange(C) // (C // 32)
    arrays = {
        "x": np.ascontiguousarray(np.asarray(x).reshape(BATCHES, C, TOK)),
        "wqkv": tiled(np.asarray(L0_conv_qkv_w).T),
        "wproj": tiled(np.asarray(L0_conv_proj_w).T),
        "bproj": np.ascontiguousarray(np.asarray(L0_conv_proj_b).reshape(CT, P).T),
        "gavg": tiled((norm_group[:, None] == norm_group[None, :]).astype(np.float32) / np.float32(C // 32)),
        "ident": np.eye(P, dtype=np.float32),
        "convw": tiled(np.asarray(L1_conv_weights)[0]),
        "coord": np.repeat(np.asarray(L1_conv_weight_coord)[0], IMG, axis=0),
        "radius": np.repeat(np.asarray(L1_conv_radius).reshape(POINTS, 1), IMG, axis=0),
        "lin_x": np.tile(lin[np.clip(delta, 0, KS - 1)], (POINTS, 1)),
        "band": np.tile(-inside.astype(np.float32), (POINTS, 1)),
        "lin_y": np.tile(lin, (P, 1)),
    }
    nc = bacc.Bacc("TRN2", target_bir_lowering=False, num_devices=1)
    given = {k: nc.dram_tensor(f"in_{k}", a.shape, F32, kind="ExternalInput").ap() for k, a in arrays.items()}
    out = nc.dram_tensor("out_y", (BATCHES, C, TOK), F32, kind="ExternalOutput").ap()
    build(nc, out=out, **given)
    r = run_bass_kernel_spmd(nc, [{f"in_{k}": a for k, a in arrays.items()}], core_ids=[0])
    return r.results[0]["out_y"].reshape(BATCHES, C, IMG, IMG)
```

```python
from contextlib import ExitStack

import concourse.bass as bass
from concourse import mybir

ALU = mybir.AluOpType
ACT = mybir.ActivationFunctionType
AX = mybir.AxisListType
F32 = mybir.dt.float32
F32R = mybir.dt.float32r

P = 128
BATCHES, C, IMG = 16, 384, 32
TOK = IMG * IMG
CT = C // P
D = 32
HG = 4
GROUPS = C // D // HG
KT = TOK // P
QN = 512
QC = TOK // QN
SCALE = float(D) ** -0.5
EPS = 1e-5
POINTS, KS = 4, 11
PAD = KS // 2
STEPS = QC * KT
SMAX = HG * KT * 2
OPEN = 2
SMAX_AT = [0, 0, 4, 5, 7, 5, 4, 7, 5, 4, 7, 5, 4, 7, 0, 0]
MAX_ROWS_AT = 15
QK_AT = (4, 7, 10, 13)
DEN_AT = 2
INVERT_AT = 4
PROB_RING = 3
PAIRS = STEPS // 2
DEN_LAG = 3
DEN_CHUNK = 1
OPEN_AT = (4, 8, 12, 16)
RECIP = 8
CHUNK_ROWS = 4
CHUNKS = CT * IMG // CHUNK_ROWS
Z_RING = 3
ZW_ROWS = 8
PIECES = CT * IMG // ZW_ROWS
V_EARLY = 2
GN1_AT = (5, 7)
GN0_AT = (16, 18)
STATS_AT = 9
GN0_PIECE = 10
GN_LINKS = [7, 8]
MEAN_READ, VAR_READ, VAR_DONE = 2, 5, 6
assert sum(SMAX_AT) == SMAX and len(SMAX_AT) == STEPS


class Batch:

    def __init__(self, n0, engine=None, turn=None, count=None):
        self.n0, self.engine, self.turn, self.count = n0, engine, turn, count

    def plus(self, k):
        return Batch(self.n0 + k, self.engine, self.turn, self.count)

    def exists(self):
        return 0 <= self.n0 < BATCHES

    def looped(self):
        return self.turn is not None

    def rising(self, per_round, c):
        if not self.looped():
            return c
        self.engine.reg_mul(self.count, self.turn, per_round)
        self.engine.reg_add(self.count, self.count, c)
        return self.count

    def of(self, per, c):
        return self.rising(2 * per, per * self.n0 + c)

    def index(self):
        return self.turn * 2 + self.n0 if self.looped() else self.n0


MISC = (
    [("smax1", 0, 0)] + [("qk2", 0, i) for i in range(4)] + [("max1", 0, 0)]
    + [("z", -1, c) for c in range(GN0_AT[0] + 2)] + [("gn0", 1, 0)]
    + [("z", -1, c) for c in range(GN0_AT[0] + 2, GN0_AT[1] + 2)] + [("gn0", 1, 1)]
    + [("z", -1, c) for c in range(GN0_AT[1] + 2, CHUNKS)]
    + [("smax2", 0, 0)] + [("qk0", 1, i) for i in range(4)] + [("max2", 0, 0)]
    + [("smax0", 1, 0)] + [("qk1", 1, i) for i in range(4)] + [("max0", 1, 0)]
    + [("v", 1, t) for t in range(V_EARLY)] + [("proj", 0, i) for i in range(CT * QC)] + [("v", 1, t) for t in range(V_EARLY, GN1_AT[0])] + [("gn1", 0, 0)]
    + [("v", 1, t) for t in range(*GN1_AT)] + [("gn1", 0, 1)] + [("v", 1, t) for t in range(GN1_AT[1], KT)]
)
MISC_BANK = {}
for at, (name, _, i) in enumerate(MISC):
    alone = name.startswith(("qk", "max"))
    MISC_BANK[name, i] = 1 if name.startswith("smax") else 0 if alone else 1 - MISC_BANK[MISC[at - 1][0], MISC[at - 1][2]]
MISC_PER_BATCH = sum(not name.startswith("smax") for name, _, _ in MISC)
MISC_END = {}
MISC_BEFORE = {}
ended, holder = 0, [None, None]
for b in range(-1, BATCHES + 1):
    for name, off, i in MISC:
        if 0 <= b + off < BATCHES:
            job = (name, b + off, i)
            ended += not name.startswith("smax")
            MISC_END[job], MISC_BEFORE[job] = ended, holder[MISC_BANK[name, i]]
            holder[MISC_BANK[name, i]] = job


def build(nc, x, out, wqkv, wproj, bproj, gavg, ident, convw, coord, radius, lin_x, band, lin_y):
    x_b = x.rearrange("b (p t) n -> b p t n", p=P)
    out_b = out.rearrange("b (p t) n -> b p t n", p=P)
    with ExitStack() as ctx:
        def sb(name, shape, dt=F32):
            return ctx.enter_context(nc.sbuf_tensor(name, shape, dt))

        def psum(name, shape):
            return ctx.enter_context(nc.psum_tensor(name, shape, F32))

        def sem(name):
            return ctx.enter_context(nc.semaphore(name))

        wqkv_s = sb("wqkv_s", [P, CT, 3 * C])
        wproj_s = sb("wproj_s", [P, CT, C])
        bproj_s = sb("bproj_s", [P, CT])
        gavg_s = sb("gavg_s", [P, P])
        ident_s = sb("ident_s", [P, P])
        convw_s = sb("convw_s", [P, CT, POINTS])
        coord_s = sb("coord_s", [P, 2])
        radius_s = sb("radius_s", [P, 1])
        lin_x_s = sb("lin_x_s", [P, IMG])
        band_s = sb("band_s", [P, IMG])
        lin_y_s = sb("lin_y_s", [P, KS])
        ones_s = sb("ones_s", [P, D])
        halfpow = sb("halfpow", [P, 1])
        tent_hi = sb("tent_hi", [P, KS, IMG], F32R)
        tent_lo = sb("tent_lo", [P, KS, IMG], F32R)
        carrier = sb("carrier", [P, 1])
        pool_carrier = sb("pool_carrier", [P, PIECES])
        tmp_x = sb("tmp_x", [P, IMG])
        tmp_y = sb("tmp_y", [P, KS])
        rinv = sb("rinv", [P, 1])
        xin = sb("xin", [P, CT, TOK])
        y = sb("y", [P, CT, TOK])
        stage = sb("stage", [P, 4, TOK], F32R)
        qp = sb("qp", [P, 2, HG, TOK], F32R)
        kp = sb("kp", [P, 2, HG, TOK], F32R)
        v = sb("v", [P, KT, C])
        probs = sb("probs", [P, PROB_RING, HG, QN])
        probsum = sb("probsum", [P, HG, QN])
        rden = sb("rden", [P, QN])
        attn = sb("attn", [P, GROUPS, TOK])
        zw = sb("zw", [P, 2, ZW_ROWS, POINTS, IMG])
        tent = zw[:, 0].rearrange("c y p x -> c (y p x)")[:, 0:KS * IMG].rearrange("c (y x) -> c y x", x=IMG)
        z_hi = sb("z_hi", [P, Z_RING, CHUNK_ROWS, P], F32R)
        z_lo = sb("z_lo", [P, Z_RING, CHUNK_ROWS, P], F32R)
        halfmax = sb("halfmax", [P, HG * KT, 2])
        negmax = sb("negmax", [P, HG * KT])
        maxrow = sb("maxrow", [HG * KT, P], F32R)
        bst = [sb(f"bst{i}", [P, CT, 2, 6]) for i in range(2)]
        mv = [sb(f"mv{i}", [P, CT, 2]) for i in range(2)]
        gmean = [sb(f"gmean{i}", [P, 1]) for i in range(2)]
        dev = [sb(f"dev{i}", [P, CT]) for i in range(2)]
        spread = [sb(f"spread{i}", [P, CT]) for i in range(2)]
        gvar = [sb(f"gvar{i}", [P, 1]) for i in range(2)]
        rstd = [sb(f"rstd{i}", [P, 1]) for i in range(2)]
        shift = [sb(f"shift{i}", [P, 1]) for i in range(2)]
        wscale = sb("wscale", [P, CT, POINTS])
        wshift = sb("wshift", [P, CT, POINTS])

        score_t = [psum(f"score_t{i}", [P, QN]) for i in range(2)]
        score_m = [psum(f"score_m{i}", [P, QN]) for i in range(2)]
        acc_o = psum("acc_o", [P, QN])
        acc_d = psum("acc_d", [P, QN])
        misc = [psum(f"misc{i}", [P, QN]) for i in range(2)]
        score_m.append(misc[1])

        loaded = sem("loaded")
        weights_loaded = sem("weights_loaded")
        consts_set = sem("consts_set")
        tent_step = sem("tent_step")
        x_loaded = sem("x_loaded")
        y_loaded = sem("y_loaded")
        stored = sem("stored")
        packed = [sem(f"packed{j}") for j in range(HG)]
        max_placed = sem("max_placed")
        misc_full = sem("misc_full")
        smax_full = sem("smax_full")
        smax_read = sem("smax_read")
        negmax_ready = sem("negmax_ready")
        maxrow_ready = sem("maxrow_ready")
        st_full = sem("st_full")
        exp_done = sem("exp_done")
        pv_done = sem("pv_done")
        probsum_ready = sem("probsum_ready")
        den_done = sem("den_done")
        acc_copied = sem("acc_copied")
        den_copied = sem("den_copied")
        rden_ready = sem("rden_ready")
        attn_ready = sem("attn_ready")
        hi_ready = sem("hi_ready")
        lo_ready = sem("lo_ready")
        v_ready = sem("v_ready")
        stats_ready = [sem(f"stats_ready{i}") for i in range(2)]
        gn_step = [sem(f"gn_step{i}") for i in range(2)]
        rstd_ready = [sem(f"rstd_ready{i}") for i in range(2)]
        xn_ready = sem("xn_ready")
        y_ready = sem("y_ready")
        zw_ready = sem("zw_ready")
        z_hi_ready = sem("z_hi_ready")
        z_lo_ready = sem("z_lo_ready")
        conv_full = sem("conv_full")
        out_ready = sem("out_ready")

        def wait_misc(e, name, n, i=0):
            e.wait_ge(misc_full, n.rising(2 * MISC_PER_BATCH, MISC_END[(name, n.n0, i)]))

        def misc_full_by(e, name, n, i=0):
            wait_misc(e, name, n, i)
            return misc[MISC_BANK[name, i]]

        def misc_bank(e, name, n, i=0):
            if MISC_BEFORE[(name, n.n0, i)]:
                before, m0, k = MISC_BEFORE[(name, n.n0, i)]
                m = n.plus(m0 - n.n0)
                if before == "v":
                    e.wait_ge(v_ready, m.of(KT, k + 1))
                elif before.startswith("qk"):
                    e.wait_ge(lo_ready, m.of(4 * GROUPS, 4 * int(before[2]) + k + 1))
                elif before.startswith("max"):
                    e.wait_ge(maxrow_ready, m.of(GROUPS, int(before[3]) + 1))
                elif before.startswith("smax"):
                    e.wait_ge(smax_read, m.of(GROUPS * SMAX, (int(before[4]) + 1) * SMAX))
                elif before.startswith("gn"):
                    e.wait_ge(gn_step[int(before[2])], m.of(GN_LINKS[int(before[2])], (MEAN_READ, VAR_READ)[k]))
                elif before == "proj":
                    e.wait_ge(y_ready, m.of(CT * QC, k + 1))
                else:
                    e.wait_ge(z_lo_ready, m.of(CHUNKS, k + 1))
            return misc[MISC_BANK[name, i]]

        def group(n, g):
            return lambda per, c=0: n.of(GROUPS * per, g * per + c)

        def slot_of(n, g):
            return (GROUPS * n.n0 + g) % 2

        def prob_slot(n, g, step):
            return ((GROUPS * n.n0 + g) * STEPS + step) % PROB_RING

        def first(n, g, before=0):
            return not n.looped() and GROUPS * n.n0 + g <= before - 1

        def run(e, iteration):
            iteration(Batch(-1))
            iteration(Batch(0))
            with e.register("count") as count, e.Fori(0, (BATCHES - 2) // 2) as turn:
                iteration(Batch(1, e, turn, count))
                iteration(Batch(2, e, turn, count))
            iteration(Batch(BATCHES - 1))
            iteration(Batch(BATCHES))

        block = ctx.enter_context(nc.Block())

        @block.sync
        def _(sp):
            for dst, src in ((gavg_s, gavg), (ident_s, ident), (bproj_s, bproj), (convw_s, convw), (coord_s, coord),
                             (radius_s, radius), (lin_x_s, lin_x), (band_s, band), (lin_y_s, lin_y)):
                sp.dma_start(dst[:], src).then_inc(loaded, 16)
            sp.dma_start(xin[:], x_b[0]).then_inc(x_loaded, 16)
            for dst, src in ((wqkv_s, wqkv), (wproj_s, wproj)):
                sp.dma_start(dst[:], src).then_inc(weights_loaded, 16)

            def load_x(n):
                wait_misc(sp, "qk2", n.plus(-1), 3)
                sp.dma_start(xin[:], x_b[n.index()]).then_inc(x_loaded, 16)

            def load_y(n):
                if n.n0 > 0:
                    sp.wait_ge(stored, n.of(16 * CT, 0))
                sp.dma_start(y[:], x_b[n.index()]).then_inc(y_loaded, 16)

            def pack(n, g):
                s, gi = slot_of(n, g), group(n, g)
                sp.wait_ge(lo_ready, gi(4, 4))
                if not first(n, g, 2):
                    sp.wait_ge(st_full, gi(STEPS * HG, -STEPS * HG))
                for j in range(HG):
                    rows = slice(D * j, D * j + D)
                    for dst, at, part in ((qp, 0, 0), (kp, 0, 2), (qp, 1, 1), (kp, 1, 2), (qp, 2, 0), (kp, 2, 3)):
                        sp.dma_start(dst[D * at:D * at + D, s, j, :].bitcast(F32), stage[rows, part, :].bitcast(F32)).then_inc(packed[j], 16)

            def place_max(n, g):
                sp.wait_ge(maxrow_ready, group(n, g)(1, 1))
                sp.dma_start(qp[3 * D:3 * D + 1, slot_of(n, g)].bitcast(F32), maxrow[:].bitcast(F32)).then_inc(max_placed, 16)

            def store(n):
                for ct in range(CT):
                    sp.wait_ge(out_ready, n.of(2 * CT, 2 * ct + 2))
                    sp.dma_start(out_b[n.index()][:, ct], y[:, ct]).then_inc(stored, 16)

            def iteration(b):
                if b.exists():
                    place_max(b, 1)
                    pack(b, 2)
                if b.exists() and b.plus(1).exists():
                    load_x(b.plus(1))
                if b.plus(-1).exists():
                    store(b.plus(-1))
                if b.exists():
                    load_y(b)
                    place_max(b, 2)
                if b.plus(1).exists():
                    pack(b.plus(1), 0)
                    place_max(b.plus(1), 0)
                    pack(b.plus(1), 1)

            run(sp, iteration)
            sp.wait_ge(stored, 16 * CT * BATCHES)

        @block.tensor
        def _(pe):
            def values(n, jobs, m=None):
                if n.exists() and 0 in jobs:
                    pe.wait_ge(xn_ready, n.of(CT, CT))
                for t in jobs:
                    if t in GN1_AT and m.exists():
                        gn(m, 1, GN1_AT.index(t))
                    if not n.exists():
                        continue
                    ps = misc_bank(pe, "v", n, t)
                    for ct in range(CT):
                        mm = pe.matmul(ps[:, 0:C], xin[:, ct, t * P:(t + 1) * P], wqkv_s[:, ct, 2 * C:3 * C],
                                       start=(ct == 0), stop=(ct == CT - 1))
                    mm.then_inc(misc_full, 1)

            def qk(n, g, i, ct):
                if first(n, g, 1) and i == 0 and ct == 0:
                    pe.wait_ge(weights_loaded, 16 * 2)
                if i == 0 and ct == 0:
                    pe.wait_ge(xn_ready, n.of(CT, CT))
                col, q = (i // 2) * C + g * P, (i % 2) * QN
                ps = misc_bank(pe, f"qk{g}", n, i) if ct == 0 else misc[MISC_BANK[f"qk{g}", i]]
                mm = pe.matmul(ps[:], wqkv_s[:, ct, col:col + P], xin[:, ct, q:q + QN],
                               start=(ct == 0), stop=(ct == CT - 1))
                if ct == CT - 1:
                    mm.then_inc(misc_full, 1)

            def max_rows(n, g):
                ps = misc_bank(pe, f"max{g}", n)
                pe.wait_ge(negmax_ready, group(n, g)(1, 1))
                pe.transpose(ps[0:HG * KT, 0:P], negmax[:], ident_s[:]).then_inc(misc_full, 1)

            def smax(n, g, k):
                j, t, half, s, gi = k // (2 * KT), k // 2 % KT, k % 2, slot_of(n, g), group(n, g)
                if k % (2 * KT) == 0:
                    pe.wait_ge(packed[j], gi(96, 96))
                if k == 2:
                    misc_bank(pe, f"smax{g}", n)
                if k >= 3 or not first(n, g, 1):
                    pe.wait_ge(smax_read, gi(SMAX, max(k - 2, 0)))
                pe.matmul(score_m[k % 3][:], qp[0:3 * D, s, j, t * P:(t + 1) * P],
                          kp[0:3 * D, s, j, half * QN:(half + 1) * QN], start=True, stop=True).then_inc(smax_full, 1)

            def scores(n, g, step, j):
                qc, t, s, gi = step // KT, step % KT, slot_of(n, g), group(n, g)
                k = step * HG + j
                if k == 0:
                    pe.wait_ge(max_placed, gi(16, 16))
                if k >= 2 or not first(n, g, 1):
                    pe.wait_ge(exp_done, gi(STEPS * HG, k - 1))
                pe.matmul(score_t[k % 2][:], kp[0:3 * D + 1, s, j, t * P:(t + 1) * P],
                          qp[0:3 * D + 1, s, j, qc * QN:(qc + 1) * QN], start=True, stop=True).then_inc(st_full, 1)

            def pv(n, g, step):
                t, gi = step % KT, group(n, g)
                pe.wait_ge(exp_done, gi(STEPS * HG, (step + 1) * HG))
                if t == 0 and not (first(n, g, 1) and step == 0):
                    pe.wait_ge(acc_copied, gi(QC, step // KT))
                if step == 0 and g == 1 and n.plus(-1).exists():
                    pe.wait_ge(out_ready, n.of(2 * CT, 0))
                if step == 0 and g == 0:
                    pe.wait_ge(v_ready, n.of(KT, KT))
                for j in range(HG):
                    h = g * HG + j
                    mm = pe.matmul(acc_o[D * j:D * j + D, :], v[:, t, h * D:(h + 1) * D],
                                   probs[:, prob_slot(n, g, step), j, :], start=(t == 0), stop=(t == KT - 1),
                                   tile_position=(0, D * j))
                mm.then_inc(pv_done, 1)

            def den(n, g, pair):
                gi, per_chunk = group(n, g), PAIRS // QC
                t = pair % per_chunk
                pe.wait_ge(probsum_ready, gi(PAIRS * HG, (pair + 1) * HG))
                if t == 0 and not (first(n, g, 1) and pair == 0):
                    pe.wait_ge(den_copied, gi(QC, pair // per_chunk))
                for j in range(HG):
                    mm = pe.matmul(acc_d[D * j:D * j + D, :], ones_s[:], probsum[:, j, :], start=(t == 0),
                                   stop=(t == per_chunk - 1), tile_position=(0, D * j))
                mm.then_inc(den_done, 1)

            def attention(n, g, m, mg, o, og):
                k = 0
                for step in range(OPEN, STEPS):
                    if m.exists() and step == MAX_ROWS_AT:
                        max_rows(m, mg)
                    pieces = ["scores", "pv", "scores", "den"]
                    if o.exists() and step in QK_AT:
                        pieces = [0, "scores", "pv", 1, "scores", "den", 2]
                    for at, piece in enumerate(pieces):
                        if piece in range(CT):
                            qk(o, og, QK_AT.index(step), piece)
                        elif n.exists():
                            if piece == "scores":
                                for j in (0, 1) if at <= 1 else (2, 3):
                                    scores(n, g, step, j)
                            elif piece == "pv":
                                pv(n, g, step - OPEN)
                            elif step >= DEN_LAG and (step - DEN_LAG) % 2 == 0:
                                den(n, g, (step - DEN_LAG) // 2)
                            elif g == 2 and step == DEN_AT:
                                den(n, 1, PAIRS - 1)
                        while m.exists() and k < sum(SMAX_AT[:step]) + SMAX_AT[step] * (at + 1) // len(pieces):
                            smax(m, mg, k)
                            k += 1

            def gn(n, i, part):
                ps = misc_bank(pe, f"gn{i}", n, part)
                pe.wait_ge(stats_ready[i], n.of(2, part + 1))
                mm = pe.matmul(ps[:, 0:CT], gavg_s[:], mv[i][:, :, 0] if part == 0 else spread[i][:], start=True, stop=True)
                mm.then_inc(misc_full, 1)

            def turn_chunk(n, c):
                ps = misc_bank(pe, "z", n, c)
                piece, row = c * CHUNK_ROWS // ZW_ROWS, c * CHUNK_ROWS % ZW_ROWS
                if row == 0:
                    pe.wait_ge(zw_ready, n.of(PIECES * POINTS, (piece + 1) * POINTS))
                for r in range(CHUNK_ROWS):
                    mm = pe.transpose(ps[:, r * P:(r + 1) * P], zw[:, piece % 2, row + r].rearrange("c p x -> c (p x)"),
                                      ident_s[:])
                mm.then_inc(misc_full, 1)

            def opening(n, g, i):
                if n.exists():
                    for j in (2 * i, 2 * i + 1):
                        scores(n, g, j // HG, j % HG)

            def after(n, g, o=None):
                for i in range(4):
                    if o:
                        opening(o, g + 1, i)
                    if i < OPEN and n.exists():
                        pv(n, g, STEPS - OPEN + i)

            def conv(n, m):
                if n.exists():
                    turn_chunk(n, 0)
                    turn_chunk(n, 1)
                after = n.plus(1)
                if n.exists():
                    pe.wait_ge(acc_copied, after.of(GROUPS * QC, QC if after.exists() else 0))
                half_rows = IMG // 2
                for c in range(CHUNKS):
                    if c in GN0_AT and m.exists():
                        gn(m, 0, GN0_AT.index(c))
                    if not n.exists():
                        continue
                    if c + 2 < CHUNKS:
                        turn_chunk(n, c + 2)
                    if c == DEN_CHUNK and after.exists():
                        den(after, 0, PAIRS - 1)
                    if c == (half_rows - PAD) // CHUNK_ROWS:
                        pe.wait_ge(den_copied, after.of(GROUPS * QC, QC if after.exists() else 0))
                    pe.wait_ge(z_lo_ready, n.of(CHUNKS, c + 1))
                    ct, row0 = c * CHUNK_ROWS // IMG, c * CHUNK_ROWS % IMG
                    if c in OPEN_AT:
                        opening(n.plus(1), 1, OPEN_AT.index(c))
                    if row0 == 0 and ct > 0:
                        pe.wait_ge(out_ready, n.of(2 * CT, 2 * ct - 1))
                    if row0 == (half_rows - PAD) // CHUNK_ROWS * CHUNK_ROWS and ct > 0:
                        pe.wait_ge(out_ready, n.of(2 * CT, 2 * ct))
                    for r in range(CHUNK_ROWS):
                        row = row0 + r
                        for half, acc in enumerate((acc_o, acc_d)):
                            lo, hi = half * half_rows, (half + 1) * half_rows
                            a, e = max(row - PAD, lo), min(row + PAD + 1, hi)
                            if a >= e:
                                continue
                            dy = a - (row - PAD)
                            for part, (zp, tp) in enumerate(((z_hi, tent_hi), (z_lo, tent_hi), (z_hi, tent_lo))):
                                mm = pe.matmul(acc[:, (a - lo) * IMG:(e - lo) * IMG], zp[:, c % Z_RING, r, :],
                                               tp[:, dy:dy + e - a, :], start=(row == max(0, lo - PAD) and part == 0),
                                               stop=(row == min(IMG, hi + PAD) - 1 and part == 2), skip_group_check=True)
                            if row == min(IMG, hi + PAD) - 1:
                                mm.then_inc(conv_full, 1)

            def proj(n, i):
                ot, qc = i % CT, i // CT
                ps = misc_bank(pe, "proj", n, i)
                if ot == 0:
                    pe.wait_ge(attn_ready, n.of(GROUPS * QC, (GROUPS - 1) * QC + qc + 1))
                for g in range(GROUPS):
                    mm = pe.matmul(ps[:], wproj_s[:, g, ot * P:(ot + 1) * P], attn[:, g, qc * QN:(qc + 1) * QN],
                                   start=(g == 0), stop=(g == GROUPS - 1))
                mm.then_inc(misc_full, 1)

            def close(n, m):
                for t in range(V_EARLY):
                    values(m, (t,))
                    opening(m, 0, t)
                for i in range(CT * QC):
                    if n.exists():
                        if i == 0:
                            den(n, 2, PAIRS - 1)
                        proj(n, i)
                    if V_EARLY + i < 4:
                        opening(m, 0, V_EARLY + i)
                values(m, range(V_EARLY, KT), n)

            pe.wait_ge(loaded, 16 * 9)
            pe.wait_ge(consts_set, 1)
            pe.wait_ge(tent_step, 10)

            def iteration(b):
                prev, nxt = b.plus(-1), b.plus(1)
                attention(b, 0, b, 1, b, 2)
                after(b, 0, None if prev.exists() else b)
                if b.exists() and not prev.exists():
                    den(b, 0, PAIRS - 1)
                conv(prev, nxt)
                attention(b, 1, b, 2, nxt, 0)
                after(b, 1, b)
                attention(b, 2, nxt, 0, nxt, 1)
                after(b, 2)
                close(b, nxt)

            run(pe, iteration)

        @block.scalar
        def _(act):
            def values(n, jobs):
                for t in jobs:
                    ps = misc_full_by(act, "v", n, t)
                    if t == 0 and n.n0 > 0:
                        act.wait_ge(pv_done, n.of(GROUPS * STEPS, 0))
                    act.copy(v[:, t, :], ps[:, 0:C]).then_inc(v_ready, 1)

            def high(n, g, i):
                ps = misc_full_by(act, f"qk{g}", n, i)
                if i == 0 and not first(n, g, 1):
                    for j in range(HG):
                        act.wait_ge(packed[j], group(n, g)(96))
                act.copy(stage[:, 2 * (i // 2), (i % 2) * QN:(i % 2 + 1) * QN], ps[:]).then_inc(hi_ready, 1)

            def exps(n, g, jobs, o=None, og=0):
                gi = group(n, g)
                for k in jobs:
                    step, j = k // HG, k % HG
                    if o and o.exists() and j == 0 and step - 1 in QK_AT:
                        high(o, og, QK_AT.index(step - 1))
                    if not n.exists():
                        continue
                    act.wait_ge(st_full, gi(STEPS * HG, k + 1))
                    if not (first(n, g, 1) and step < PROB_RING):
                        if j == 0:
                            act.wait_ge(pv_done, gi(STEPS, step - PROB_RING + 1))
                        act.wait_ge(probsum_ready, gi(PAIRS * HG, (step - PROB_RING) // 2 * HG + j + 1))
                    act.activation(probs[:, prob_slot(n, g, step), j, :], score_t[k % 2][:], ACT.Exp,
                                   scale=SCALE).then_inc(exp_done, 1)
                    if g == 2 and (step, j) == (DEN_AT, HG - 1):
                        copy_den(n, 1, 1)
                    if (step, j) == (KT + OPEN - 1, 1):
                        copy_acc(n, g, 0)
                    if (step, j) == (KT + DEN_LAG - 1, HG - 1):
                        copy_den(n, g, 0)

            def copy_acc(n, g, qc):
                gi = group(n, g)
                act.wait_ge(pv_done, gi(STEPS, (qc + 1) * KT))
                act.copy(attn[:, g, qc * QN:(qc + 1) * QN], acc_o[:]).then_inc(acc_copied, 1)

            def copy_den(n, g, qc):
                gi = group(n, g)
                act.wait_ge(den_done, gi(PAIRS, (qc + 1) * PAIRS // QC))
                if not (first(n, g, 1) and qc == 0):
                    act.wait_ge(attn_ready, gi(QC, qc))
                act.copy(rden[:], acc_d[:]).then_inc(den_copied, 1)

            def z_high(n):
                for c in range(CHUNKS):
                    ps = misc_full_by(act, "z", n, c)
                    act.copy(z_hi[:, c % Z_RING], ps[:].rearrange("q (y c) -> q y c", c=P)).then_inc(z_hi_ready, 1)
                    if c == DEN_CHUNK + 2 and n.plus(1).exists():
                        copy_den(n.plus(1), 0, 1)
                    if c - 2 in OPEN_AT:
                        opening(n.plus(1), 1, OPEN_AT.index(c - 2))

            def opening(n, g, i):
                if n.exists():
                    exps(n, g, (2 * i, 2 * i + 1))

            def attention(n, g, o, og):
                exps(n, g, range(OPEN * HG, STEPS * HG), o, og)

            def after(n, g, o=None):
                for i in range(4):
                    if o:
                        opening(o, g + 1, i)
                if n.exists():
                    copy_acc(n, g, 1)

            def iteration(b):
                prev, nxt = b.plus(-1), b.plus(1)
                attention(b, 0, b, 2)
                after(b, 0, None if prev.exists() else b)
                if prev.exists():
                    z_high(prev)
                elif b.exists():
                    copy_den(b, 0, 1)
                attention(b, 1, nxt, 0)
                after(b, 1, b)
                attention(b, 2, nxt, 1)
                after(b, 2)
                for i in range(4):
                    if i < V_EARLY and nxt.exists():
                        values(nxt, (i,))
                    if i == V_EARLY and b.exists():
                        copy_den(b, 2, 1)
                    opening(nxt, 0, i)
                if nxt.exists():
                    values(nxt, range(V_EARLY, KT))

            run(act, iteration)

        @block.gpsimd
        def _(pool):
            def rstd_of(n, i):
                pool.wait_ge(gn_step[i], n.of(GN_LINKS[i], VAR_DONE))
                pool.tensor_tensor(rstd[i][:], gvar[i][:], halfpow[:], ALU.pow).then_inc(rstd_ready[i], 1)

            def weigh(n, pieces, m=None):
                if n.exists() and 0 in pieces:
                    pool.wait_ge(gn_step[1], n.of(GN_LINKS[1], GN_LINKS[1]))
                for piece in pieces:
                    if piece == GN0_PIECE + 1 and m.exists():
                        rstd_of(m, 0)
                    if not n.exists():
                        continue
                    ct, row = piece * ZW_ROWS // IMG, piece * ZW_ROWS % IMG
                    if piece >= 2 or n.n0 > 0:
                        last = ((piece - 1) * ZW_ROWS // CHUNK_ROWS - 1) % CHUNKS
                        wait_misc(pool, "z", n if piece >= 2 else n.plus(-1), last)
                    pool.tensor_tensor(pool_carrier[:, piece:piece + 1], halfpow[:], halfpow[:], ALU.add)
                    for p in range(POINTS):
                        pool.tensor_scalar(zw[:, piece % 2, :, p, :],
                                           y[:, ct, row * IMG:(row + ZW_ROWS) * IMG].rearrange("c (y x) -> c y x", x=IMG),
                                           wscale[:, ct, p:p + 1], wshift[:, ct, p:p + 1], ALU.mult,
                                           ALU.add).then_inc(zw_ready, 1)

            def add_pairs(n, g, pairs):
                gi = group(n, g)
                for pair in pairs:
                    for j in range(HG):
                        pool.wait_ge(exp_done, gi(STEPS * HG, (2 * pair + 1) * HG + j + 1))
                        if j == 0 and not (first(n, g, 1) and pair == 0):
                            pool.wait_ge(den_done, gi(PAIRS, pair))
                        pool.tensor_tensor(probsum[:, j, :], probs[:, prob_slot(n, g, 2 * pair), j, :],
                                           probs[:, prob_slot(n, g, 2 * pair + 1), j, :],
                                           ALU.add).then_inc(probsum_ready, 1)

            def divide(n, g, qc):
                part = attn[:, g, qc * QN:(qc + 1) * QN]
                pool.wait_ge(rden_ready, group(n, g)(QC * RECIP, (qc + 1) * RECIP))
                pool.tensor_tensor(part, part, rden[:], ALU.mult).then_inc(attn_ready, 1)

            pool.wait_ge(consts_set, 1)

            def iteration(b):
                prev, nxt = b.plus(-1), b.plus(1)
                if b.exists():
                    add_pairs(b, 0, range(0, 2))
                weigh(prev, range(0, 2))
                if b.exists():
                    add_pairs(b, 0, range(2, PAIRS - 1))
                    divide(b, 0, 0)
                    add_pairs(b, 0, (PAIRS - 1,))
                weigh(prev, range(2, PIECES), nxt)
                if b.exists():
                    divide(b, 0, 1)
                if b.exists():
                    add_pairs(b, 1, range(0, PAIRS - 1))
                    divide(b, 1, 0)
                    add_pairs(b, 1, (PAIRS - 1,))
                    add_pairs(b, 2, range(0, 4))
                    divide(b, 1, 1)
                    add_pairs(b, 2, range(4, PAIRS - 1))
                    divide(b, 2, 0)
                    add_pairs(b, 2, (PAIRS - 1,))
                    divide(b, 2, 1)
                    rstd_of(b, 1)

            run(pool, iteration)

        @block.vector
        def _(dve):
            def link(ins, step, count):
                ins.then_inc(step, 1)
                dve.wait_ge(step, count)

            dve.memset(halfpow[:], -0.5)
            dve.memset(kp[3 * D:3 * D + 1].bitcast(F32), 1.0)
            dve.memset(ones_s[:], 1.0).then_inc(consts_set, 1)
            dve.wait_ge(loaded, 16 * 9)
            link(dve.tensor_scalar(tmp_x[:], lin_x_s[:], coord_s[:, 0:1], None, ALU.subtract), tent_step, 1)
            link(dve.scalar_tensor_tensor(out=tmp_x[:], in0=tmp_x[:], scalar=-1.0, in1=tmp_x[:],
                                          op0=ALU.mult, op1=ALU.max), tent_step, 2)
            link(dve.tensor_scalar(tmp_y[:], lin_y_s[:], coord_s[:, 1:2], None, ALU.subtract), tent_step, 3)
            link(dve.scalar_tensor_tensor(out=tmp_y[:], in0=tmp_y[:], scalar=-1.0, in1=tmp_y[:],
                                          op0=ALU.mult, op1=ALU.max), tent_step, 4)
            link(dve.reciprocal(rinv[:], radius_s[:]), tent_step, 5)
            link(dve.tensor_tensor(tent, tmp_x[:].unsqueeze(1).to_broadcast([P, KS, IMG]),
                                   tmp_y[:].unsqueeze(2).to_broadcast([P, KS, IMG]), ALU.add), tent_step, 6)
            link(dve.tensor_scalar(tent, tent, rinv[:], -1.0, ALU.mult, ALU.add), tent_step, 7)
            link(dve.scalar_tensor_tensor(out=tent, in0=tent, scalar=0.0,
                                          in1=band_s[:].unsqueeze(1).to_broadcast([P, KS, IMG]),
                                          op0=ALU.min, op1=ALU.mult), tent_step, 8)
            link(dve.tensor_copy(tent_hi[:], tent), tent_step, 9)
            dve.tensor_tensor(tent_lo[:], tent, tent_hi[:].bitcast(F32), ALU.subtract).then_inc(tent_step, 1)

            def channel_stats(n, i, parts=range(CT * 2)):
                src = xin if i == 0 else y
                if i == 0:
                    dve.wait_ge(x_loaded, n.of(16, 16))
                else:
                    dve.wait_ge(y_ready, n.of(CT * QC, CT * QC))
                for part in parts:
                    ct, h = part // 2, part % 2
                    ins = dve.bn_stats(bst[i][:, ct, h, :], src[:, ct, h * QN:(h + 1) * QN])
                if CT * 2 - 1 not in parts:
                    return
                link(ins, gn_step[i], n.of(GN_LINKS[i], 1))
                dve.memset(carrier[:], 0.0)
                for ct in range(CT):
                    ins = dve.bn_aggr(mv[i][:, ct, :], bst[i][:, ct].rearrange("c h s -> c (h s)"))
                ins.then_inc(stats_ready[i], 1)

            def norm_mean(n, i):
                ps = misc_full_by(dve, f"gn{i}", n, 0)
                link(dve.tensor_reduce(gmean[i][:], ps[:, 0:CT], AX.X, ALU.add), gn_step[i], n.of(GN_LINKS[i], MEAN_READ))
                link(dve.tensor_tensor(dev[i][:], mv[i][:, :, 0], gmean[i][:].to_broadcast([P, CT]), ALU.subtract),
                     gn_step[i], n.of(GN_LINKS[i], 3))
                link(dve.tensor_tensor(dev[i][:], dev[i][:], dev[i][:], ALU.mult), gn_step[i], n.of(GN_LINKS[i], 4))
                dve.tensor_tensor(spread[i][:], dev[i][:], mv[i][:, :, 1], ALU.add).then_inc(stats_ready[i], 1)

            def norm_var(n, i):
                ps = misc_full_by(dve, f"gn{i}", n, 1)
                link(dve.tensor_reduce(gvar[i][:], ps[:, 0:CT], AX.X, ALU.add), gn_step[i], n.of(GN_LINKS[i], VAR_READ))
                link(dve.tensor_scalar(gvar[i][:], gvar[i][:], EPS, None, ALU.add), gn_step[i], n.of(GN_LINKS[i], VAR_DONE))

            def norm_shift(n, i):
                dve.wait_ge(rstd_ready[i], n.of(1, 1))
                link(dve.scalar_tensor_tensor(out=shift[i][:], in0=gmean[i][:], scalar=-1.0, in1=rstd[i][:],
                                              op0=ALU.mult, op1=ALU.mult), gn_step[i], n.of(GN_LINKS[i], 7))

            def norm_x(n, ct):
                dve.tensor_scalar(xin[:, ct], xin[:, ct], rstd[0][:, 0:1], shift[0][:, 0:1], ALU.mult, ALU.add).then_inc(xn_ready, 1)

            def norm_weights(n):
                dve.tensor_tensor(wscale[:], convw_s[:], rstd[1][:].unsqueeze(2).to_broadcast([P, CT, POINTS]), ALU.mult)
                dve.tensor_tensor(wshift[:], convw_s[:], shift[1][:].unsqueeze(2).to_broadcast([P, CT, POINTS]),
                                  ALU.mult).then_inc(gn_step[1], 1)

            def read_max(n, g, k):
                dve.wait_ge(smax_full, group(n, g)(SMAX, k + 1))
                dve.tensor_reduce(halfmax[:, k // 2, k % 2:k % 2 + 1], score_m[k % 3][:], AX.X,
                                  ALU.max).then_inc(smax_read, 1)

            def combine_max(n, g):
                dve.wait_ge(smax_read, group(n, g)(SMAX, SMAX))
                dve.tensor_reduce(negmax[:], halfmax[:], AX.X, ALU.max, negate=True).then_inc(negmax_ready, 1)

            def max_rows(n, g):
                ps = misc_full_by(dve, f"max{g}", n)
                if not first(n, g, 1):
                    dve.wait_ge(max_placed, group(n, g)(16))
                dve.tensor_copy(maxrow[:], ps[0:HG * KT, 0:P]).then_inc(maxrow_ready, 1)

            def invert(n, g, qc, pieces):
                gi, width = group(n, g), QN // RECIP
                for i in pieces:
                    dve.wait_ge(den_copied, gi(QC, qc + 1))
                    part = rden[:, i * width:(i + 1) * width]
                    dve.reciprocal(part, part).then_inc(rden_ready, 1)

            def attention(n, g, m, mg, o, og):
                k = 0
                for step in range(STEPS):
                    for i in range(SMAX_AT[step] if m.exists() else 0):
                        read_max(m, mg, k)
                        k += 1
                        if k == SMAX:
                            combine_max(m, mg)
                    if o.exists() and step in QK_AT:
                        low(o, og, QK_AT.index(step))
                    if n.exists() and g == 2 and 0 <= step - INVERT_AT < RECIP // 2:
                        invert(n, 1, 1, (2 * (step - INVERT_AT), 2 * (step - INVERT_AT) + 1))
                    if n.exists() and 0 <= step - KT - DEN_LAG < RECIP // 2:
                        invert(n, g, 0, (2 * (step - KT - DEN_LAG), 2 * (step - KT - DEN_LAG) + 1))
                    if m.exists() and step == MAX_ROWS_AT:
                        max_rows(m, mg)

            def low(n, g, i):
                bank = MISC_BANK[f"qk{g}", i]
                part = stage[:, 2 * (i // 2):2 * (i // 2) + 2, (i % 2) * QN:(i % 2 + 1) * QN]
                dve.wait_ge(hi_ready, group(n, g)(4, i + 1))
                dve.tensor_tensor(part[:, 1], misc[bank][:], part[:, 0].bitcast(F32), ALU.subtract).then_inc(lo_ready, 1)

            def residual(n, i):
                if i == 0:
                    dve.wait_ge(y_loaded, n.of(16, 16))
                ot, qc = i % CT, i // CT
                ps = misc_full_by(dve, "proj", n, i)
                part = y[:, ot, qc * QN:(qc + 1) * QN]
                dve.scalar_tensor_tensor(out=part, in0=ps[:], scalar=bproj_s[:, ot:ot + 1], in1=part,
                                         op0=ALU.add, op1=ALU.add).then_inc(y_ready, 1)

            def z_low(n, c):
                bank = misc[MISC_BANK["z", c]]
                dve.wait_ge(z_hi_ready, n.of(CHUNKS, c + 1))
                dve.tensor_tensor(z_lo[:, c % Z_RING], bank[:].rearrange("q (y c) -> q y c", c=P),
                                  z_hi[:, c % Z_RING].bitcast(F32), ALU.subtract).then_inc(z_lo_ready, 1)

            def outputs(n, ct, half):
                dve.wait_ge(conv_full, n.of(2 * CT, 2 * ct + half + 1))
                part = y[:, ct, half * QN:(half + 1) * QN]
                dve.tensor_tensor(part, (acc_o, acc_d)[half][:], part, ALU.add).then_inc(out_ready, 1)

            def conv(n, m):
                for c in range(CHUNKS):
                    if n.exists():
                        z_low(n, c)
                    if m.exists():
                        if STATS_AT <= c < STATS_AT + CT * 2:
                            channel_stats(m, 0, (c - STATS_AT,))
                        elif c == GN0_AT[0] + 1:
                            norm_mean(m, 0)
                        elif c == GN0_AT[1] + 1:
                            norm_var(m, 0)
                        elif c >= CHUNKS - CT:
                            if c == CHUNKS - CT:
                                norm_shift(m, 0)
                            norm_x(m, c - (CHUNKS - CT))
                    if not n.exists():
                        continue
                    if n.plus(1).exists() and 4 <= c < 4 + RECIP:
                        invert(n.plus(1), 0, 1, (c - 4,))
                    ct, row = divmod((c - 2) * CHUNK_ROWS, IMG)
                    if c >= 2 and row <= IMG // 2 + PAD - 1 < row + CHUNK_ROWS:
                        outputs(n, ct, 0)
                    if c >= 2 and row == IMG - CHUNK_ROWS:
                        outputs(n, ct, 1)
                if n.exists():
                    outputs(n, CT - 1, 1)

            def iteration(b):
                prev, nxt = b.plus(-1), b.plus(1)
                attention(b, 0, b, 1, b, 2)
                if b.exists() and not prev.exists():
                    invert(b, 0, 1, range(RECIP))
                conv(prev, nxt)
                attention(b, 1, b, 2, nxt, 0)
                attention(b, 2, nxt, 0, nxt, 1)
                if b.exists():
                    invert(b, 2, 1, range(RECIP))
                    for i in range(CT * QC):
                        residual(b, i)
                    channel_stats(b, 1)
                    norm_mean(b, 1)
                    norm_var(b, 1)
                    norm_shift(b, 1)
                    norm_weights(b)

            run(dve, iteration)


def kernel(x, L0_conv_qkv_w, L0_conv_proj_w, L0_conv_proj_b, L1_conv_weight_coord, L1_conv_radius, L1_conv_weights):
    import numpy as np
    import concourse.bacc as bacc
    from concourse.bass_utils import run_bass_kernel_spmd

    def tiled(w):
        w = np.asarray(w)
        return np.ascontiguousarray(w.reshape(P, CT, -1))

    lin = np.linspace(-1.0, 1.0, KS).astype(np.float32)
    delta = np.arange(IMG)[:, None] - np.arange(IMG)[None, :] + PAD
    inside = (delta >= 0) & (delta < KS)
    norm_group = np.arange(P) // (P // 32)
    wproj = np.asarray(L0_conv_proj_w).T.reshape(CT, P, P, CT)
    arrays = {
        "x": np.ascontiguousarray(np.asarray(x).reshape(BATCHES, C, TOK)),
        "wqkv": tiled(np.asarray(L0_conv_qkv_w).T),
        "wproj": np.ascontiguousarray(wproj.transpose(1, 0, 3, 2).reshape(P, CT, C)),
        "bproj": np.ascontiguousarray(np.asarray(L0_conv_proj_b).reshape(P, CT)),
        "gavg": (norm_group[:, None] == norm_group[None, :]).astype(np.float32) / np.float32(C // 32),
        "ident": np.eye(P, dtype=np.float32),
        "convw": tiled(np.asarray(L1_conv_weights)[0]),
        "coord": np.repeat(np.asarray(L1_conv_weight_coord)[0], IMG, axis=0),
        "radius": np.repeat(np.asarray(L1_conv_radius).reshape(POINTS, 1), IMG, axis=0),
        "lin_x": np.tile(lin[np.clip(delta, 0, KS - 1)], (POINTS, 1)),
        "band": np.tile(-inside.astype(np.float32), (POINTS, 1)),
        "lin_y": np.tile(lin, (P, 1)),
    }
    nc = bacc.Bacc("TRN2", target_bir_lowering=False, num_devices=1, dynamic_dma_scratch_size=1024)
    given = {k: nc.dram_tensor(f"in_{k}", a.shape, F32, kind="ExternalInput").ap() for k, a in arrays.items()}
    out = nc.dram_tensor("out_y", (BATCHES, C, TOK), F32, kind="ExternalOutput").ap()
    build(nc, out=out, **given)
    r = run_bass_kernel_spmd(nc, [{f"in_{k}": a for k, a in arrays.items()}], core_ids=[0])
    return r.results[0]["out_y"].reshape(BATCHES, C, IMG, IMG)
```
